# Optimizing a Trainium2 kernel written in Bass

```python
import numpy as np
import jax
import jax.numpy as jnp

def _softmax(x, axis=-1):
    return jax.nn.softmax(x, axis=axis)

def _gelu(x):
    return jax.nn.gelu(x, approximate=True)

def _silu(x):
    return jax.nn.silu(x)

def _sigmoid(x):
    return jax.nn.sigmoid(x)

def _layernorm(x, axis=-1, eps=1e-05):
    m = jnp.mean(x, axis=axis, keepdims=True)
    v = jnp.var(x, axis=axis, keepdims=True)
    return (x - m) / jnp.sqrt(v + eps)

def _scatter_add(tgt, idx, src, axis=0):
    return tgt.at[idx].add(src)

def _segment_sum(src, seg, n):
    return jax.ops.segment_sum(src, seg, n)
kernel_name = 'mk_seq_preln_d1_jaxref_r4_629980'

def setup_inputs(seed: int=0):
    np.random.seed(seed)
    _w = jnp.asarray

    def _L0_attn_setup():
        import jax, jax.numpy as jnp
        import numpy as np
        HID = 512
        HEADS = 16
        HD = HID // HEADS
        EPS = 1e-06

        def _heads(x, b, s):
            return x.reshape(b, s, HEADS, HD).transpose(0, 2, 1, 3)
        key = jax.random.key(seed)
        ks = jax.random.split(key, 9)
        s = 1.0 / np.sqrt(HID)
        return {'hidden_states': jax.random.normal(ks[0], (4, 1024, HID), jnp.float32), 'q_w': jax.random.normal(ks[1], (HID, HID), jnp.float32) * s, 'q_b': jnp.zeros((HID,), jnp.float32), 'k_w': jax.random.normal(ks[2], (HID, HID), jnp.float32) * s, 'k_b': jnp.zeros((HID,), jnp.float32), 'v_w': jax.random.normal(ks[3], (HID, HID), jnp.float32) * s, 'v_b': jnp.zeros((HID,), jnp.float32), 'o_w': jax.random.normal(ks[4], (HID, HID), jnp.float32) * s, 'o_b': jnp.zeros((HID,), jnp.float32)}
    _L0_attn_in = _L0_attn_setup()

    def _L0_ffn_setup():
        import math
        import jax, jax.numpy as jnp
        import numpy as np
        NUM_EXPERTS = 8
        TOP_K = 2
        CAP_FACTOR = 1.25
        D_MODEL = 512
        D_HIDDEN = 2048
        B, S = (4, 512)
        key = jax.random.key(seed)
        ks = jax.random.split(key, 6)
        x = jax.random.normal(ks[0], (B, S, D_MODEL), dtype=jnp.float32)
        gating_w = jax.random.normal(ks[1], (D_MODEL, NUM_EXPERTS), dtype=jnp.float32) * (1.0 / math.sqrt(D_MODEL))
        w1 = jax.random.normal(ks[2], (NUM_EXPERTS, D_MODEL, D_HIDDEN), dtype=jnp.float32) * (1.0 / math.sqrt(D_MODEL))
        b1 = jnp.zeros((NUM_EXPERTS, D_HIDDEN), dtype=jnp.float32)
        w2 = jax.random.normal(ks[3], (NUM_EXPERTS, D_HIDDEN, D_MODEL), dtype=jnp.float32) * (1.0 / math.sqrt(D_HIDDEN))
        b2 = jnp.zeros((NUM_EXPERTS, D_MODEL), dtype=jnp.float32)
        return {'x': x, 'gating_w': gating_w, 'w1': w1, 'b1': b1, 'w2': w2, 'b2': b2}
    _L0_ffn_in = _L0_ffn_setup()
    _d = {'L0_attn_hidden_states': _L0_attn_in['hidden_states'], 'L0_attn_q_w': _L0_attn_in['q_w'], 'L0_attn_q_b': _L0_attn_in['q_b'], 'L0_attn_k_w': _L0_attn_in['k_w'], 'L0_attn_k_b': _L0_attn_in['k_b'], 'L0_attn_v_w': _L0_attn_in['v_w'], 'L0_attn_v_b': _L0_attn_in['v_b'], 'L0_attn_o_w': _L0_attn_in['o_w'], 'L0_attn_o_b': _L0_attn_in['o_b'], 'L0_ffn_gating_w': _L0_ffn_in['gating_w'], 'L0_ffn_w1': _L0_ffn_in['w1'], 'L0_ffn_b1': _L0_ffn_in['b1'], 'L0_ffn_w2': _L0_ffn_in['w2'], 'L0_ffn_b2': _L0_ffn_in['b2']}
    _x0 = _d['L0_attn_hidden_states']
    _d['L0_attn_hidden_states'] = jax.random.normal(jax.random.fold_in(jax.random.key(seed), 1), (4, 1024, 512), dtype=_x0.dtype)
    del _x0
    return _d

def reference(L0_attn_hidden_states, L0_attn_q_w, L0_attn_q_b, L0_attn_k_w, L0_attn_k_b, L0_attn_v_w, L0_attn_v_b, L0_attn_o_w, L0_attn_o_b, L0_ffn_gating_w, L0_ffn_w1, L0_ffn_b1, L0_ffn_w2, L0_ffn_b2):

    def _L0_attn_ref(hidden_states, q_w, q_b, k_w, k_b, v_w, v_b, o_w, o_b):
        import jax, jax.numpy as jnp
        import numpy as np
        HID = 512
        HEADS = 16
        HD = HID // HEADS
        EPS = 1e-06

        def _heads(x, b, s):
            return x.reshape(b, s, HEADS, HD).transpose(0, 2, 1, 3)
        b, s, _ = hidden_states.shape
        q = _heads(hidden_states @ q_w.T + q_b, b, s)
        k = _heads(hidden_states @ k_w.T + k_b, b, s)
        v = _heads(hidden_states @ v_w.T + v_b, b, s)
        qp = jax.nn.elu(q) + 1.0
        kp = jax.nn.elu(k) + 1.0
        kv = jnp.einsum('bhsd,bhse->bhde', kp, v)
        z = jnp.einsum('bhsd,bhd->bhs', qp, kp.sum(axis=2))[..., None]
        attn = jnp.einsum('bhsd,bhde->bhse', qp, kv) / (z + EPS)
        out = attn.transpose(0, 2, 1, 3).reshape(b, s, HID)
        return out @ o_w.T + o_b

    def _L0_ffn_ref(x, gating_w, w1, b1, w2, b2):
        import math
        import jax, jax.numpy as jnp
        import numpy as np
        NUM_EXPERTS = 8
        TOP_K = 2
        CAP_FACTOR = 1.25
        D_MODEL = 512
        D_HIDDEN = 2048
        B, S = (4, 512)
        b, s, d = x.shape
        x_flat = x.reshape(-1, d)
        T = x_flat.shape[0]
        num_items = T * TOP_K
        capacity = int(math.ceil(num_items / NUM_EXPERTS * CAP_FACTOR))
        gates = jax.nn.softmax(x_flat @ gating_w, axis=-1)
        topk_w, topk_idx = jax.lax.top_k(gates, TOP_K)
        norm_w = topk_w / (jnp.sum(topk_w, axis=-1, keepdims=True) + 1e-08)
        flat_e = topk_idx.reshape(-1)
        flat_t = jnp.repeat(jnp.arange(T, dtype=jnp.int32), TOP_K)
        flat_w = norm_w.reshape(-1)
        onehot = (flat_e[:, None] == jnp.arange(NUM_EXPERTS)[None, :]).astype(jnp.int32)
        pos_all = jnp.cumsum(onehot, axis=0) - 1
        position = jnp.take_along_axis(pos_all, flat_e[:, None].astype(jnp.int32), axis=1)[:, 0]
        valid = position < capacity
        pos_scatter = jnp.where(valid, position, capacity)
        buf = jnp.zeros((NUM_EXPERTS, capacity, d), dtype=x.dtype)
        buf = buf.at[flat_e, pos_scatter].set(x_flat[flat_t], mode='drop')
        h = jnp.maximum(jnp.einsum('ecd,edh->ech', buf, w1) + b1[:, None, :], 0.0)
        out_e = jnp.einsum('ech,ehd->ecd', h, w2) + b2[:, None, :]
        pos_gather = jnp.minimum(position, capacity - 1)
        gathered = out_e[flat_e, pos_gather]
        w_eff = jnp.where(valid, flat_w, 0.0)
        out_flat = jnp.zeros_like(x_flat).at[flat_t].add(gathered * w_eff[:, None])
        return out_flat.reshape(b, s, d)
    x = L0_attn_hidden_states
    x = x + _L0_attn_ref(_layernorm(x, axis=-1), L0_attn_q_w, L0_attn_q_b, L0_attn_k_w, L0_attn_k_b, L0_attn_v_w, L0_attn_v_b, L0_attn_o_w, L0_attn_o_b)
    x = x + _L0_ffn_ref(_layernorm(x, axis=-1), L0_ffn_gating_w, L0_ffn_w1, L0_ffn_b1, L0_ffn_w2, L0_ffn_b2)
    return x

_drawn_inputs = setup_inputs


def setup_inputs(seed=0):
    import zlib

    import numpy as np

    out = dict(_drawn_inputs(seed))
    spreads = {'L0_attn_q_b': (0.0, 0.685),
     'L0_attn_k_b': (0.0, 0.8),
     'L0_attn_v_b': (0.0, 0.1),
     'L0_attn_o_b': (0.0, 0.1),
     'L0_ffn_b1': (0.0, 0.1),
     'L0_ffn_b2': (0.0, 0.1)}
    factors = {'L0_attn_q_w': 3.376}
    for name, (base, spread) in spreads.items():
        noise = np.random.default_rng([zlib.crc32(name.encode()), seed]).standard_normal(out[name].shape)
        drawn = base * np.exp(spread * noise) if base else spread * noise
        out[name] = jnp.asarray(drawn.astype(out[name].dtype))
    for name, factor in factors.items():
        out[name] = (out[name] * factor).astype(out[name].dtype)
    return out
```

```python
from contextlib import ExitStack

import concourse.bass as bass
from concourse import mybir

F32 = mybir.dt.float32
F32R = mybir.dt.float32r
I32 = mybir.dt.int32
ALU = mybir.AluOpType
ACT = mybir.ActivationFunctionType
AX = mybir.AxisListType

P = 128
HEAD_DIM = 32
LN_EPS = 1e-5
Z_EPS = 1e-6
W_EPS = 1e-8
CAPACITY_NUM, CAPACITY_DEN = 5, 4
TOP_K = 2
PAD = 256


def moe_block(nc, x_in, wq_t, bq, wk_t, bk, wv_t, bv, wo_t, bo, gate_w, w1, b1, w2, b2, out):
    B, S, D = x_in.shape
    E, _, HID = w1.shape
    T = B * S
    NT = S // P
    KC = D // P
    G = KC
    HPG = P // HEAD_DIM
    CAP = T * TOP_K * CAPACITY_NUM // (E * CAPACITY_DEN)
    SLOTS = E * CAP
    TT = 256
    HT = TT // P
    TPE = CAP // TT
    MC = HID // P
    PAIRS = MC // 2
    HB = S // 512
    R = NT * E
    ROUTE_STEPS = 38 + NT
    RING = 4
    assert CAP % TT == 0 and D == 512 and HB == 2 and NT == 8

    xrows = x_in.rearrange("b (t p) d -> b t p d", p=P)
    out_t = out[0:T, :].rearrange("(b t p) d -> b t p d", b=B, p=P)
    normed = nc.dram_tensor("normed", [T + PAD, D], F32).ap()
    normed_t = normed[0:T, :].rearrange("(b t p) d -> b t p d", b=B, p=P)
    table = nc.dram_tensor("slot_table", [SLOTS, 2], F32).ap()
    table_t = table.rearrange("(g h p) c -> g p h c", h=HT, p=P)

    ctx = ExitStack()
    with ctx:
        def sb(name, shape, dt=F32, scope=ctx):
            return scope.enter_context(nc.sbuf_tensor(name, shape, dt))

        def sem(name):
            return ctx.enter_context(nc.semaphore(name))

        bank = [ctx.enter_context(nc.psum_tensor(f"bank{i}", [P, 512], F32)) for i in range(8)]

        stage = sb("stage", [P, 2, 2048])
        ident = sb("ident", [P, P])
        plan_f = sb("plan_f", [P, 2, E + 1])
        plan = sb("plan", [P, 2, E + 1], I32)
        EXTRA, BEFORE = range(2)

        pa = ExitStack()
        sa = lambda name, shape, dt=F32: sb(name, shape, dt, pa)
        whi = {c: sa(f"w{c}_hi", [P, KC, D], F32R) for c in "kvqo"}
        wlo = {c: sa(f"w{c}_lo", [P, KC, D], F32R) for c in "kvqo"}
        xb = sa("xb", [P, NT, D])
        xt_hi = sa("xt_hi", [P, KC, S], F32R)
        xt_lo = sa("xt_lo", [P, KC, S], F32R)
        qp = sa("qp", [P, KC, S])
        xn = sa("xn", [P, 2, D])
        kt = sa("kt", [P, D])
        ke = sa("ke", [P, D])
        kp = sa("kp", [P, 2, D])
        vx = sa("vx", [P, 2, G, P + 1])
        qt = sa("qt", [P, 512])
        qe = sa("qe", [P, 512])
        bkb = sa("bkb", [P, D])
        bvb = sa("bvb", [P, D])
        bob = sa("bob", [P, D])
        bqt = sa("bqt", [P, KC])
        kvd = sa("kvd", [P, G, P])
        ksd = sa("ksd", [P, G, HPG])
        at = sa("at", [P, D])
        at_hi = sa("at_hi", [P, KC, P], F32R)
        at_lo = sa("at_lo", [P, KC, P], F32R)
        x1 = sa("x1", [P, 2, D])
        x1n = sa("x1n", [P, 2, D])
        nt = sa("nt", [P, KC, P])
        gw = sa("gw", [P, KC, E])
        stats = sa("stats", [P, 2, 6])
        mv = sa("mv", [P, 2, 2])
        ve = sa("ve", [P, 2])
        rstd = sa("rstd", [P, 2])
        stats2 = sa("stats2", [P, 6])
        mv2 = sa("mv2", [P, 2])
        ve2 = sa("ve2", [P, 1])
        rstd2 = sa("rstd2", [P, 1])
        nhalf = sa("nhalf", [P, 1])
        zi = sa("zi", [P, 2, G * HPG])
        headmask = sa("headmask", [P, HPG, HEAD_DIM])
        upper = sa("upper", [P, P])
        ones = sa("ones", [P, P])
        zrow = sa("zrow", [P, D])
        tabinit_i = sa("tabinit_i", [P, SLOTS // P], I32)
        tabinit = sa("tabinit", [P, SLOTS // P, 2])
        tok_id = sa("tok_id", [P, T // P], I32)
        ei = sa("ei", [P, E], I32)
        ef = sa("ef", [P, E])
        ecap = sa("ecap", [P, E])
        lg = sa("lg", [P, NT, E])
        gt = sa("gt", [P, NT, E])
        tmp = sa("tmp", [P, NT, E])
        oh = sa("oh", [P, 2, NT, E])
        cnt = sa("cnt", [P, NT, E])
        pos = sa("pos", [P, NT, E])
        base = sa("base", [P, NT + 1, E])
        m = sa("m", [P, 8, NT])
        slot_i = sa("slot_i", [P, 2, NT], I32)
        rec = sa("rec", [P, 2, NT, 2])
        RM, RS, G1, G2, I1, WS, VA, SL = range(8)

        n_ = sem
        x_landed = [n_(f"x_landed{i}") for i in range(NT)]
        st_landed = [n_(f"st_landed{i}") for i in range(2)]
        small_landed = n_("small_landed")
        const_done, const_set, mask_cut = n_("const_done"), n_("const_set"), n_("mask_cut")
        dconst_done, tab_zeroed, base_zeroed = n_("dconst_done"), n_("tab_zeroed"), n_("base_zeroed")
        zrow_stored = n_("zrow_stored")
        tab_stored = n_("tab_stored")
        st_hi, st_lo = n_("st_hi"), n_("st_lo")
        stats_done, mv_done, ve_done, rstd_done = n_("stats_done"), n_("mv_done"), n_("ve_done"), n_("rstd_done")
        xn_done, bo_added = n_("xn_done"), n_("bo_added")
        tr_full, tr_hi, tr_lo = n_("tr_full"), n_("tr_hi"), n_("tr_lo")
        k_full, kt_done, km_done, ke_done, kp_done = n_("k_full"), n_("kt_done"), n_("km_done"), n_("ke_done"), n_("kp_done")
        v_full, v_done = n_("v_full"), n_("v_done")
        kv_acc = n_("kv_acc")
        kvd_done = n_("kvd_done")
        q_full, qt_done, qm_done, qe_done, qp_done = n_("q_full"), n_("qt_done"), n_("qm_done"), n_("qe_done"), n_("qp_done")
        num_full, z_read, z_rec, at_done = n_("num_full"), n_("z_read"), n_("z_rec"), n_("at_done")
        o_full, x1_done = n_("o_full"), n_("x1_done")
        x1_stored = [n_(f"x1_stored{i}") for i in range(2)]
        stats2_done, mv2_done, ve2_done, rstd2_done, x1n_done = n_("stats2_done"), n_("mv2_done"), n_("ve2_done"), n_("rstd2_done"), n_("x1n_done")
        x1n_stored = [n_(f"x1n_stored{i}") for i in range(2)]
        nt_full, nt_done = n_("nt_full"), n_("nt_done")
        lg_full = n_("lg_full")
        route = n_("route")
        lg_exp_in, lg_exp = n_("lg_exp_in"), n_("lg_exp")
        cnt_done, cum_full = n_("cnt_done"), n_("cum_full")
        rec_done = n_("rec_done")
        ids_done = n_("ids_done")
        scattered = [n_(f"scattered{i}") for i in range(4)]
        recs_free = n_("recs_free")
        phase_a = n_("phase_a")

        pb = ExitStack()

        T0 = NT + 4
        STEPS = T0 + NT + 5

        carrier = n_("carrier")
        planned, plan_ready = n_("planned"), n_("plan_ready")

        def carry(eng):
            eng.sem_inc(carrier, 1)

        def tiles_of(eng, e):
            e_ = slice(e, e + 1) if isinstance(e, int) else bass.ds(e, 1)
            return (eng.value_load(plan[0:1, EXTRA, e_], min_val=0, max_val=TPE - 1),
                    eng.value_load(plan[0:1, BEFORE, e_], min_val=0, max_val=E * TPE))

        def staged(eng, n):
            eng.wait_ge(st_landed[n % 2], 16 * (n // 2 + 1))

        def alloc_b():
            names = {}
            b = lambda name, shape, dt=F32: names.__setitem__(name, sb(name, shape, dt, pb))
            b("w1_hi", [P, KC, HID], F32R)
            b("w1_lo", [P, KC, HID], F32R)
            b("w2_hi", [P, MC, D], F32R)
            b("w2_lo", [P, MC, D], F32R)
            b("stage2", [P, RING, 1024])
            b("xg", [P, HT, D])
            b("et_hi", [P, KC, TT], F32R)
            b("et_lo", [P, KC, TT], F32R)
            b("h32", [P, 2, TT])
            b("h_hi", [P, 4, TT], F32R)
            b("h_lo", [P, 4, TT], F32R)
            b("ys", [P, HT, D])
            b("b1_all", [P, E, MC])
            b("b1_cur", [P, MC])
            b("b2_cur", [P, D])
            b("tab_g", [P, HT, 2])
            b("tab_s", [P, HT, 2])
            return names

        pa.close()
        nb = alloc_b()
        w1_hi, w1_lo, w2_hi, w2_lo = (nb[k] for k in ("w1_hi", "w1_lo", "w2_hi", "w2_lo"))
        stage2 = nb["stage2"]
        stage1 = stage[:].rearrange("p a (b c) -> p (a b) c", c=1024)
        xg, et_hi, et_lo, h32, h_hi, h_lo = (nb[k] for k in ("xg", "et_hi", "et_lo", "h32", "h_hi", "h_lo"))
        ys, b1_all, b1_cur, b2_cur, tab_g, tab_s = (nb[k] for k in ("ys", "b1_all", "b1_cur", "b2_cur", "tab_g", "tab_s"))
        w1_landed = [n_(f"w1_landed{i}") for i in range(RING)]
        w2_landed = [n_(f"w2_landed{i}") for i in range(RING)]
        w1_split_hi, w1_ready = n_("w1_split_hi"), n_("w1_ready")
        w2_split_hi, w2_ready = n_("w2_split_hi"), n_("w2_ready")
        b1_landed, b1_copied = n_("b1_landed"), n_("b1_copied")
        b2_landed = n_("b2_landed")
        tabg_landed, tabs_landed = n_("tabg_landed"), n_("tabs_landed")
        gathered = [n_(f"gathered{i}") for i in range(HT)]
        added = [n_(f"added{i}") for i in range(HT)]
        adds_done = n_("adds_done")
        et_full, et_split_hi, et_ready = n_("et_full"), n_("et_split_hi"), n_("et_ready")
        h_full, h32_done, h_split_hi, h_ready = n_("h_full"), n_("h32_done"), n_("h_split_hi"), n_("h_ready")
        mm2_done = n_("mm2_done")
        y_read, y_done = n_("y_read"), n_("y_done")
        ctx.enter_context(pb)

        h_bank = bank[0:4]
        et_bank = bank[4:6]
        y_bank = bank[6:8]
        LAG = 2

        block = ctx.enter_context(nc.Block())

        @block.sync
        def _(sp):
            def load_x(b, i):
                sp.dma_start(xb[:, i, :], xrows[b, i] if isinstance(b, int) else
                             xrows[bass.ds(b, 1), i].rearrange("a p d -> (a p) d")).then_inc(x_landed[i], 16)

            for i in range(2):
                sp.sem_inc(x1_stored[i], 16)
                sp.sem_inc(x1n_stored[i], 16)
            for i in range(2):
                load_x(0, i)
            for n, w in enumerate((wk_t, wv_t)):
                sp.dma_start(stage[:, n, :].rearrange("p (c d) -> p c d", c=KC),
                             w.rearrange("(c p) d -> p c d", p=P)).then_inc(st_landed[n], 16)
            sp.dma_start(bkb[:], bk.partition_broadcast(P)).then_inc(small_landed, 16)
            sp.dma_start(bvb[:], bv.partition_broadcast(P)).then_inc(small_landed, 16)
            sp.dma_start(bob[:], bo.partition_broadcast(P)).then_inc(small_landed, 16)
            sp.dma_start(gw[:], gate_w.rearrange("(c p) e -> p c e", p=P)).then_inc(small_landed, 16)
            with nc.allow_non_contiguous_dma(reason="512 biases"):
                sp.dma_start(bqt[:], bq.rearrange("(c p) -> p c", p=P)).then_inc(small_landed, 16)
            for i in range(2, NT):
                load_x(0, i)
            for n, w in ((2, wq_t), (3, wo_t)):
                sp.wait_ge(st_lo, n - 1)
                sp.dma_start(stage[:, n % 2, :].rearrange("p (c d) -> p c d", c=KC),
                             w.rearrange("(c p) d -> p c d", p=P)).then_inc(st_landed[n % 2], 16)
            sp.wait_ge(dconst_done, 2)
            for r in range(PAD // P):
                sp.dma_start(normed[T + r * P:T + (r + 1) * P, :], zrow[:]).then_inc(zrow_stored, 16)
                sp.dma_start(out[T + r * P:T + (r + 1) * P, :], zrow[:]).then_inc(zrow_stored, 16)
            sp.dma_start(table.rearrange("(p s) c -> p s c", p=P), tabinit[:]).then_inc(tab_stored, 16)

            def batch(b, last):
                for i in range(NT):
                    v = NT * b + i
                    sp.wait_ge(x1_done, v + 1)
                    sp.dma_start(out_t[bass.ds(b, 1), i].rearrange("a p d -> (a p) d"), x1[:, i % 2, :]) \
                        .then_inc(x1_stored[i % 2], 16)
                    if not last:
                        sp.dma_start(xb[:, i, :], xrows[bass.ds(b + 1, 1), i].rearrange("a p d -> (a p) d")) \
                            .then_inc(x_landed[i], 16)
                    sp.wait_ge(x1n_done, v + 1)
                    sp.dma_start(normed_t[bass.ds(b, 1), i].rearrange("a p d -> (a p) d"), x1n[:, i % 2, :]) \
                        .then_inc(x1n_stored[i % 2], 16)

            with sp.Fori(0, B - 1) as b:
                batch(b, False)
            batch(B - 1, True)
            for i in range(2):
                sp.wait_ge(x1_stored[i], 16 * (T // P // 2 + 1))
                sp.wait_ge(x1n_stored[i], 16 * (T // P // 2 + 1))

            def load_w1(e, j):
                sp.wait_ge(w1_ready, PAIRS * e + j + 1)
                w1v = w1[e] if isinstance(e, int) else w1[bass.ds(e, 1)].rearrange("a d h -> (a d) h")
                sp.dma_start(stage1[:, j % RING, :].rearrange("p (c h) -> p c h", c=KC),
                             w1v[:, 256 * j:256 * (j + 1)].rearrange("(c p) h -> p c h", p=P)) \
                    .then_inc(w1_landed[j % RING], 16)

            def load_w2(e, j):
                sp.wait_ge(w2_ready, PAIRS * e + j + 1)
                w2v = w2[e] if isinstance(e, int) else w2[bass.ds(e, 1)].rearrange("a h d -> (a h) d")
                sp.dma_start(stage2[:, j % RING, :].rearrange("p (c d) -> p c d", c=2),
                             w2v[256 * j:256 * (j + 1), :].rearrange("(c p) d -> p c d", p=P)) \
                    .then_inc(w2_landed[j % RING], 16)

            def load_tab_g(g):
                sp.dma_start(tab_g[:], table_t[bass.ds(g, 1)].rearrange("a p h c -> (a p) h c")
                             if not isinstance(g, int) else table_t[g]).then_inc(tabg_landed, 16)

            def load_tab_s(g):
                sp.dma_start(tab_s[:], table_t[bass.ds(g, 1)].rearrange("a p h c -> (a p) h c")
                             if not isinstance(g, int) else table_t[g]).then_inc(tabs_landed, 16)

            sp.wait_ge(st_lo, 4)
            for j in range(RING):
                load_w1(0, j)
            sp.wait_ge(phase_a, 4)
            with nc.allow_non_contiguous_dma(reason="biases laid out by partition"):
                sp.dma_start(b1_all[:], b1.rearrange("e (c p) -> p e c", p=P)).then_inc(b1_landed, 16)
            load_tab_g(0)
            for j in range(RING):
                load_w2(0, j)
            for j in range(RING, PAIRS):
                load_w1(0, j)
                load_w2(0, j)

            def tile_loads(g, n, following):
                sp.wait_ge(adds_done, g + 1)
                load_tab_s(n)
                if following is not None:
                    for h in range(HT):
                        sp.wait_ge(gathered[h], 16 * (g + 1))
                    load_tab_g(following)

            def load_b2(e, before):
                sp.wait_ge(y_read, HT * before + 1)
                b2v = b2[e:e + 1, :] if isinstance(e, int) else b2[bass.ds(e, 1), :]
                sp.dma_start(b2_cur[:], b2v.rearrange("a d -> (a d)").partition_broadcast(P)).then_inc(b2_landed, 16)

            def expert(e, more):
                extra, before = tiles_of(sp, e)
                load_b2(e, before)
                if more:
                    for j in range(RING):
                        load_w1(e + 1, j)
                        load_w2(e + 1, j)
                with sp.Fori(0, TPE - 1) as t:
                    with sp.If(t < extra):
                        tile_loads(before + t, e * TPE + t, e * TPE + t + 1)
                tile_loads(before + extra, e * TPE + extra, (e + 1) * TPE if more else None)
                if more:
                    for j in range(RING, PAIRS + 2):
                        if j < PAIRS:
                            load_w1(e + 1, j)
                        if j >= RING + 2:
                            load_w2(e + 1, j - 2)

            with sp.Fori(0, E - 1) as e:
                expert(e, True)
            expert(E - 1, False)

        @block.gpsimd
        def _(pool):
            nc.gpsimd.memset(ident[:], 0.0).then_inc(const_set, 1)
            nc.gpsimd.memset(headmask[:], 1.0).then_inc(const_set, 1)
            nc.gpsimd.memset(upper[:], 1.0).then_inc(const_set, 1)
            nc.gpsimd.memset(nhalf[:], -0.5).then_inc(const_set, 1)
            nc.gpsimd.iota(tabinit_i[:], [[1, SLOTS // P]], base=0, channel_multiplier=SLOTS // P).then_inc(ids_done, 1)
            nc.gpsimd.iota(tok_id[:], [[P, T // P]], base=0, channel_multiplier=1).then_inc(ids_done, 1)
            nc.gpsimd.iota(ei[:], [[1, E]], base=0, channel_multiplier=0).then_inc(ids_done, 1)
            pool.wait_ge(const_set, 4)
            nc.gpsimd.affine_select(out=ident[:], in_=ident[:], compare_op=ALU.not_equal, fill=1.0, base=0,
                                    pattern=[[-1, P]], channel_multiplier=1).then_inc(const_done, 1)
            nc.gpsimd.affine_select(out=headmask[:], in_=headmask[:], compare_op=ALU.is_ge, fill=0.0, base=0,
                                    pattern=[[-HEAD_DIM, HPG], [0, HEAD_DIM]], channel_multiplier=1).then_inc(mask_cut, 1)
            nc.gpsimd.affine_select(out=upper[:], in_=upper[:], compare_op=ALU.is_ge, fill=0.0, base=-1,
                                    pattern=[[1, P]], channel_multiplier=-1).then_inc(const_done, 1)
            pool.wait_ge(mask_cut, 1)
            nc.gpsimd.affine_select(out=headmask[:], in_=headmask[:], compare_op=ALU.is_ge, fill=0.0,
                                    base=HEAD_DIM - 1, pattern=[[HEAD_DIM, HPG], [0, HEAD_DIM]],
                                    channel_multiplier=-1).then_inc(const_done, 1)
            pool.wait_ge(small_landed, 80)

            def norm_scale(v, done, var, tmp_, out_, step_done, ready):
                pool.wait_ge(done, v + 1)
                carry(pool)
                nc.gpsimd.tensor_scalar(tmp_, var, LN_EPS, None, ALU.add).then_inc(step_done, 1)
                pool.wait_ge(step_done, v + 1)
                nc.gpsimd.tensor_tensor(out_, tmp_, nhalf[:], ALU.pow).then_inc(ready, 1)

            def batch(b):
                for s in range(STEPS):
                    if s < NT:
                        v = NT * b + s
                        norm_scale(v, mv_done, mv[:, s % 2, 1:2], ve[:, s % 2:s % 2 + 1], rstd[:, s % 2:s % 2 + 1],
                                   ve_done, rstd_done)
                    i = s - 1
                    if 0 <= i < NT:
                        v = NT * b + i
                        pool.wait_ge(xn_done, v + 1)
                        nc.gpsimd.tensor_tensor(xb[:, i, :], xb[:, i, :], bob[:], ALU.add).then_inc(bo_added, 1)
                    i = s - T0 - 2
                    if 0 <= i < NT:
                        v = NT * b + i
                        norm_scale(v, mv2_done, mv2[:, 1:2], ve2[:], rstd2[:], ve2_done, rstd2_done)
                pool.wait_ge(rec_done, b + 1)
                carry(pool)
                for i in range(NT):
                    for c in range(TOP_K):
                        nc.gpsimd.indirect_dma_start(
                            out=table, out_offset=bass.IndirectOffsetOnAxis(ap=slot_i[:, c, i:i + 1], axis=0),
                            in_=rec[:, c, i, :], in_offset=None, bounds_check=SLOTS - 1, oob_is_err=False,
                        ).then_inc(scattered[(TOP_K * i + c) % 4], 16)
                for q in range(4):
                    pool.wait_ge(scattered[q], 16 * (TOP_K * NT // 4) * (b + 1))
                pool.sem_inc(recs_free, 1)

            pool.sem_inc(recs_free, 1)
            pool.wait_ge(tab_stored, 16)
            with pool.Fori(0, B) as b:
                batch(b)
            pool.wait_ge(zrow_stored, 64)
            for i in range(2):
                pool.wait_ge(x1n_stored[i], 16 * (T // P // 2 + 1))
                pool.wait_ge(x1_stored[i], 16 * (T // P // 2 + 1))
            pool.drain().then_inc(phase_a, 1)

            def gather(g):
                pool.wait_ge(tabg_landed, 16 * (g + 1))
                pool.wait_ge(et_full, HT * g + 1)
                carry(pool)
                for h in range(HT):
                    nc.gpsimd.indirect_dma_start(
                        out=xg[:, h, :], out_offset=None, in_=normed,
                        in_offset=bass.IndirectOffsetOnAxis(ap=tab_g[:, h, 0:1].bitcast(I32), axis=0),
                    ).then_inc(gathered[h], 16)

            def add_rows(g):
                pool.wait_ge(y_done, HT * (g + 1))
                carry(pool)
                for h in range(HT):
                    nc.gpsimd.indirect_dma_start(
                        out=out, out_offset=bass.IndirectOffsetOnAxis(ap=tab_s[:, h, 0:1].bitcast(I32), axis=0),
                        in_=ys[:, h, :], in_offset=None, compute_op=ALU.add,
                    ).then_inc(added[h], 16)
                for h in range(HT):
                    pool.wait_ge(added[h], 16 * (g + 1))
                pool.sem_inc(adds_done, 1)

            pool.wait_ge(phase_a, 4)
            pool.sem_inc(adds_done, 1)
            gather(0)

            def expert(e, more):
                extra, before = tiles_of(pool, e)
                with pool.Fori(0, TPE - 1) as t:
                    with pool.If(t < extra):
                        gather(before + t + 1)
                        add_rows(before + t)
                if more:
                    gather(before + extra + 1)
                add_rows(before + extra)

            with pool.Fori(0, E - 1) as e:
                expert(e, True)
            expert(E - 1, False)

        @block.scalar
        def _(act):
            for n, c in enumerate("kvqo"):
                staged(act, n)
                nc.scalar.activation(whi[c][:], stage[:, n % 2, :].rearrange("p (c d) -> p c d", c=KC),
                                     ACT.Copy).then_inc(st_hi, 1)
            act.wait_ge(small_landed, 80)
            act.sem_inc(qt_done, 1)
            act.sem_inc(h32_done, 4)

            def split_hi(use, dst):
                act.wait_ge(tr_full, use + 1)
                nc.scalar.activation(dst, bank[0][:].rearrange("p (c t) -> p c t", c=KC), ACT.Copy).then_inc(tr_hi, 1)

            def batch(b):
                for s in range(STEPS):
                    i = s - 2
                    if 0 <= i < NT:
                        split_hi(2 * NT * b + i, xt_hi[:, :, P * i:P * (i + 1)])
                    c = s - 6
                    if 0 <= c < HB * KC:
                        v = HB * KC * b + c
                        act.wait_ge(q_full, v + 1)
                        act.wait_ge(qp_done, v + 1)
                        nc.scalar.activation(qt[:], bank[3][:], ACT.Identity, bias=bqt[:, c % KC:c % KC + 1]) \
                            .then_inc(qt_done, 1)
                        act.wait_ge(qm_done, v + 1)
                        nc.scalar.activation(qe[:], qe[:], ACT.Exp).then_inc(qe_done, 1)
                    i = s - 3
                    if 0 <= i < NT:
                        act.wait_ge(km_done, NT * b + i + 1)
                        nc.scalar.activation(ke[:], ke[:], ACT.Exp).then_inc(ke_done, 1)
                    i = s - T0 - 1
                    if 0 <= i < NT:
                        v = NT * b + i
                        act.wait_ge(o_full, v + 1)
                        split_hi(2 * NT * b + NT + i, at_hi[:])
                    i = s - T0 - 4
                    if 0 <= i < NT:
                        v = NT * b + i
                        act.wait_ge(nt_full, v + 1)
                        act.wait_ge(lg_full, v + 1)
                        nc.scalar.activation(nt[:], bank[7][:].rearrange("p (c t) -> p c t", c=KC), ACT.Copy) \
                            .then_inc(nt_done, 1)
                act.wait_ge(lg_exp_in, b + 1)
                nc.scalar.activation(gt[:], gt[:], ACT.Exp).then_inc(lg_exp, 1)

            with act.Fori(0, B) as b:
                batch(b)
            act.drain().then_inc(phase_a, 1)

            def w1_split(e, j):
                act.wait_ge(w1_landed[j % RING], 16 * (e * PAIRS // RING + j // RING + 1) if isinstance(e, int)
                            else e * (16 * PAIRS // RING) + 16 * (j // RING + 1))
                nc.scalar.activation(w1_hi[:, :, 256 * j:256 * (j + 1)],
                                     stage1[:, j % RING, :].rearrange("p (c h) -> p c h", c=KC), ACT.Copy) \
                    .then_inc(w1_split_hi, 1)

            def w2_split(e, j):
                act.wait_ge(w2_landed[j % RING], 16 * (e * PAIRS // RING + j // RING + 1) if isinstance(e, int)
                            else e * (16 * PAIRS // RING) + 16 * (j // RING + 1))
                nc.scalar.activation(w2_hi[:, 2 * j:2 * j + 2, :],
                                     stage2[:, j % RING, :].rearrange("p (c d) -> p c d", c=2), ACT.Copy) \
                    .then_inc(w2_split_hi, 1)

            def w2_used(g, j):
                act.wait_ge(mm2_done, MC * g + 2 * j + 2 + 4)

            def rows_hi(g):
                if not (isinstance(g, int) and g == 0):
                    act.wait_ge(h_full, MC * g)
                for c in range(2):
                    act.wait_ge(et_full, 2 * g + c + 2)
                    nc.scalar.activation(et_hi[:, 2 * c:2 * c + 2, :], et_bank[c][:].rearrange("p (c t) -> p c t", c=2),
                                         ACT.Copy).then_inc(et_split_hi, 1)

            def y_weight(g):
                act.wait_ge(tabs_landed, 16 * (g + 1))
                for h in range(HT):
                    act.wait_ge(y_read, HT * g + h + 2)
                    nc.scalar.activation(ys[:, h, :], ys[:, h, :], ACT.Copy, scale=tab_s[:, h, 1:2]) \
                        .then_inc(y_done, 1)

            def tile(e, g, final, more):
                for mm in range(MC):
                    v = MC * g + mm
                    act.wait_ge(h_full, v + 1)
                    act.wait_ge(h_ready, v + 1)
                    nc.scalar.activation(h32[:, mm % 2, :], h_bank[mm % 4][:, 0:TT], ACT.Relu,
                                         bias=b1_cur[:, mm:mm + 1]).then_inc(h32_done, 1)
                    if final and more and mm % 2 == 1:
                        j = mm // 2
                        w1_split(e + 1, j)
                        if j >= 2:
                            w2_used(g, j - 2)
                            w2_split(e + 1, j - 2)
                if more or not final:
                    rows_hi(g + 1)
                if final and more:
                    w2_used(g, PAIRS - 2)
                    w2_split(e + 1, PAIRS - 2)
                y_weight(g)
                if final and more:
                    w2_split(e + 1, PAIRS - 1)

            def b1_load(e, before):
                src = b1_all[:, e, :] if isinstance(e, int) else b1_all[:, bass.ds(e, 1), :].rearrange("p a c -> p (a c)")
                act.wait_ge(h32_done, MC * before + 4)
                carry(act)
                nc.scalar.activation(b1_cur[:], src, ACT.Copy).then_inc(b1_copied, 1)
                act.wait_ge(b1_copied, e + 1)
                carry(act)

            act.wait_ge(phase_a, 4)
            for j in range(PAIRS):
                w1_split(0, j)
                w2_split(0, j)
            act.wait_ge(b1_landed, 16)
            rows_hi(0)

            def expert(e, more):
                extra, before = tiles_of(act, e)
                b1_load(e, before)
                with act.Fori(0, TPE - 1) as t:
                    with act.If(t < extra):
                        tile(e, before + t, False, more)
                tile(e, before + extra, True, more)

            with act.Fori(0, E - 1) as e:
                expert(e, True)
            expert(E - 1, False)

        @block.vector
        def _(dve):
            ve_ = nc.vector
            dve.sem_inc(qp_done, 1)
            dve.sem_inc(tr_lo, 1)
            dve.sem_inc(z_read, 1)
            dve.sem_inc(at_done, 1)
            dve.sem_inc(kt_done, 1)
            dve.sem_inc(kp_done, 1)
            dve.sem_inc(v_done, 1)
            dve.sem_inc(w1_ready, RING)
            dve.sem_inc(w2_ready, RING)
            dve.sem_inc(h_ready, 2)
            dve.sem_inc(y_read, 1)
            ve_.memset(ones[:], 1.0)
            ve_.memset(zrow[:], 0.0).then_inc(dconst_done, 1)
            ve_.memset(tabinit[:], 0.0).then_inc(tab_zeroed, 1)
            ve_.memset(vx[:, :, :, P:P + 1], 1.0)
            ve_.memset(base[:, NT, :], 0.0).then_inc(base_zeroed, 1)
            dve.wait_ge(base_zeroed, 1)
            dve.wait_ge(ids_done, 3)
            dve.wait_ge(tab_zeroed, 1)
            ve_.tensor_scalar(tabinit[:, :, 0].bitcast(I32), tabinit_i[:], PAD - 1, T, ALU.bitwise_and, ALU.bitwise_or) \
                .then_inc(dconst_done, 1)
            ve_.tensor_copy(ef[:], ei[:]).then_inc(ids_done, 1)
            dve.wait_ge(ids_done, 4)
            ve_.tensor_scalar(ecap[:], ef[:], float(CAP), None, ALU.mult).then_inc(ids_done, 1)
            dve.wait_ge(ids_done, 5)
            for n, c in enumerate("kvqo"):
                dve.wait_ge(st_hi, n + 1)
                ve_.tensor_tensor(wlo[c][:], stage[:, n % 2, :].rearrange("p (c d) -> p c d", c=KC),
                                  whi[c][:].bitcast(F32), ALU.subtract).then_inc(st_lo, 1)
            dve.wait_ge(small_landed, 80)
            dve.wait_ge(const_done, 3)

            def split_lo(use, dst, hi):
                dve.wait_ge(tr_hi, use + 1)
                ve_.tensor_tensor(dst, bank[0][:].rearrange("p (c t) -> p c t", c=KC), hi.bitcast(F32),
                                  ALU.subtract).then_inc(tr_lo, 1)

            def batch(b):
                for s in range(STEPS):
                    if s == T0:
                        dve.wait_ge(kv_acc, NT * (b + 1) + 2)
                        hm = headmask[:].rearrange("p h c -> p (h c)")
                        for r in range(2):
                            acc = bank[4 + r][:, 0:2 * (P + 1)].rearrange("p (g c) -> p g c", g=2)
                            ve_.tensor_tensor(kvd[:, 2 * r:2 * r + 2, :], acc[:, :, 0:P],
                                              hm.unsqueeze(1).to_broadcast([P, 2, P]), ALU.mult)
                            last = ve_.tensor_tensor(ksd[:, 2 * r:2 * r + 2, :],
                                                     acc[:, :, P:P + 1].to_broadcast([P, 2, HPG]),
                                                     headmask[:, :, 0].unsqueeze(1).to_broadcast([P, 2, HPG]), ALU.mult)
                            last.then_inc(kvd_done, 1)
                    i = s
                    if i < NT:
                        v = NT * b + i
                        dve.wait_ge(x_landed[i], 16 * (b + 1))
                        if i >= 2:
                            dve.wait_ge(xn_done, v - 1)
                        ve_.bn_stats(stats[:, i % 2, :], xb[:, i, :]).then_inc(stats_done, 1)
                        dve.wait_ge(stats_done, v + 1)
                        carry(dve)
                        ve_.bn_aggr(mv[:, i % 2, :], stats[:, i % 2, :]).then_inc(mv_done, 1)
                    i = s - 1
                    if 0 <= i < NT:
                        v = NT * b + i
                        dve.wait_ge(rstd_done, v + 1)
                        if i >= 2:
                            dve.wait_ge(tr_full, 2 * NT * b + i - 1)
                        ve_.tensor_scalar(xn[:, i % 2, :], xb[:, i, :], mv[:, i % 2, 0:1], rstd[:, i % 2:i % 2 + 1],
                                          ALU.subtract, ALU.mult).then_inc(xn_done, 1)
                    i = s - 2
                    if 0 <= i < NT:
                        split_lo(2 * NT * b + i, xt_lo[:, :, P * i:P * (i + 1)], xt_hi[:, :, P * i:P * (i + 1)])
                    c = s - 6
                    if 0 <= c < HB * KC:
                        v = HB * KC * b + c
                        dve.wait_ge(qt_done, v + 2)
                        dve.wait_ge(qp_done, v + 1)
                        ve_.tensor_scalar(qe[:], qt[:], 0.0, None, ALU.min).then_inc(qm_done, 1)
                    i = s - 3
                    if 0 <= i < NT:
                        v = NT * b + i
                        dve.wait_ge(k_full, v + 1)
                        dve.wait_ge(kp_done, v + 1)
                        ve_.tensor_tensor(kt[:], bank[1][:], bkb[:], ALU.add).then_inc(kt_done, 1)
                        dve.wait_ge(kt_done, v + 2)
                        ve_.tensor_scalar(ke[:], kt[:], 0.0, None, ALU.min).then_inc(km_done, 1)
                        dve.wait_ge(v_full, v + 1)
                        dve.wait_ge(kv_acc, v + 1)
                        ve_.tensor_tensor(vx[:, i % 2, :, 0:P], bank[2][:].rearrange("p (g c) -> p g c", g=G),
                                          bvb[:].rearrange("p (g c) -> p g c", g=G), ALU.add).then_inc(v_done, 1)
                    c = s - 6
                    if 0 <= c < HB * KC:
                        v = HB * KC * b + c
                        dve.wait_ge(qe_done, v + 1)
                        ve_.scalar_tensor_tensor(out=qp[:, c % KC, 512 * (c // KC):512 * (c // KC + 1)], in0=qt[:],
                                                 scalar=0.0, in1=qe[:], op0=ALU.max, op1=ALU.add).then_inc(qp_done, 1)
                    i = s - 3
                    if 0 <= i < NT:
                        v = NT * b + i
                        dve.wait_ge(ke_done, v + 1)
                        ve_.scalar_tensor_tensor(out=kp[:, i % 2, :], in0=kt[:], scalar=0.0, in1=ke[:],
                                                 op0=ALU.max, op1=ALU.add).then_inc(kp_done, 1)
                    i = s - T0
                    if 0 <= i < NT:
                        v = NT * b + i
                        dve.wait_ge(num_full, v + 1)
                        ve_.tensor_scalar(zi[:, 0, :], bank[4][:, 0:G * HPG], Z_EPS, None, ALU.add).then_inc(z_read, 1)
                        dve.wait_ge(z_read, v + 2)
                        dve.wait_ge(at_done, v + 1)
                        ve_.reciprocal(zi[:, 1, :], zi[:, 0, :]).then_inc(z_rec, 1)
                        dve.wait_ge(z_rec, v + 1)
                        dve.wait_ge(tr_full, 2 * NT * b + NT + i)
                        ve_.tensor_tensor(at[:].rearrange("p (h c) -> p h c", c=HEAD_DIM),
                                          bank[6][:].rearrange("p (h c) -> p h c", c=HEAD_DIM),
                                          zi[:, 1, :].unsqueeze(2).to_broadcast([P, G * HPG, HEAD_DIM]), ALU.mult) \
                            .then_inc(at_done, 1)
                    i = s - T0 - 1
                    if 0 <= i < NT:
                        split_lo(2 * NT * b + NT + i, at_lo[:], at_hi[:])
                    i = s - T0 - 3
                    if 0 <= i < NT:
                        v = NT * b + i
                        dve.wait_ge(rstd2_done, v + 1)
                        dve.wait_ge(x1n_stored[i % 2], 16 * (NT // 2 * b + i // 2 + 1))
                        if i >= 2:
                            dve.wait_ge(nt_full, v - 1)
                        ve_.tensor_scalar(x1n[:, i % 2, :], x1[:, i % 2, :], mv2[:, 0:1], rstd2[:], ALU.subtract,
                                          ALU.mult).then_inc(x1n_done, 1)
                    i = s - T0 - 2
                    if 0 <= i < NT:
                        v = NT * b + i
                        dve.wait_ge(o_full, v + 2)
                        if i > 0:
                            dve.wait_ge(x1n_done, v)
                        dve.wait_ge(bo_added, v + 1)
                        dve.wait_ge(x1_stored[i % 2], 16 * (NT // 2 * b + i // 2 + 1))
                        ve_.tensor_tensor(x1[:, i % 2, :], bank[1 + i % 2][:], xb[:, i, :], ALU.add).then_inc(x1_done, 1)
                        dve.wait_ge(x1_done, v + 1)
                        ve_.bn_stats(stats2[:], x1[:, i % 2, :]).then_inc(stats2_done, 1)
                        dve.wait_ge(stats2_done, v + 1)
                        carry(dve)
                        ve_.bn_aggr(mv2[:], stats2[:]).then_inc(mv2_done, 1)
                routing(b)

            def routing(b):
                k = [0]
                r0 = ROUTE_STEPS * b

                def step(ins):
                    k[0] += 1
                    ins.then_inc(route, 1)
                    dve.wait_ge(route, r0 + k[0])

                def col(c):
                    return m[:, c, :]

                def wide(ap):
                    return ap.unsqueeze(2).to_broadcast([P, NT, E])

                efw = ef[:].unsqueeze(1).to_broadcast([P, NT, E])
                dve.wait_ge(lg_full, NT * (b + 1) + 1)
                dve.wait_ge(recs_free, b + 1)
                step(ve_.tensor_copy(lg[:], bank[5][:, 0:R].rearrange("p (t e) -> p t e", e=E)))
                step(ve_.tensor_reduce(col(RM), lg[:], AX.X, ALU.max))
                ve_.tensor_tensor(gt[:], lg[:], wide(col(RM)), ALU.subtract).then_inc(lg_exp_in, 1)
                dve.wait_ge(lg_exp, b + 1)
                step(ve_.tensor_reduce(col(RS), gt[:], AX.X, ALU.add))
                step(ve_.reciprocal(col(WS), col(RS)))
                step(ve_.tensor_tensor(gt[:], gt[:], wide(col(WS)), ALU.mult))
                for c in range(TOP_K):
                    gcol = col(G1 + c)
                    step(ve_.tensor_reduce(gcol, gt[:], AX.X, ALU.max))
                    step(ve_.tensor_tensor(tmp[:], gt[:], wide(gcol), ALU.not_equal))
                    step(ve_.scalar_tensor_tensor(out=tmp[:], in0=tmp[:], scalar=float(E), in1=efw, op0=ALU.mult,
                                                  op1=ALU.add))
                    step(ve_.tensor_reduce(col(I1), tmp[:], AX.X, ALU.min))
                    step(ve_.tensor_tensor(oh[:, c], efw, wide(col(I1)), ALU.is_equal))
                    if c == 0:
                        step(ve_.scalar_tensor_tensor(out=gt[:], in0=oh[:, 0], scalar=-2.0, in1=gt[:], op0=ALU.mult,
                                                      op1=ALU.add))
                ve_.tensor_tensor(cnt[:], oh[:, 0], oh[:, 1], ALU.add).then_inc(cnt_done, 1)
                step(ve_.tensor_copy(base[:, 0, :], base[:, NT, :]))
                dve.wait_ge(cum_full, b + 1)
                for t in range(NT):
                    step(ve_.tensor_tensor(base[:, t + 1, :], base[:, t, :], bank[5][:, 2 * R + E * t:2 * R + E * (t + 1)],
                                           ALU.add))
                step(ve_.tensor_tensor(pos[:], bank[5][:, R:2 * R].rearrange("p (t e) -> p t e", e=E),
                                       base[:, 0:NT, :], ALU.add))
                step(ve_.tensor_tensor(col(WS), col(G1), col(G2), ALU.add))
                step(ve_.tensor_scalar(col(WS), col(WS), W_EPS, None, ALU.add))
                step(ve_.reciprocal(col(WS), col(WS)))
                for c in range(TOP_K):
                    step(ve_.tensor_tensor(tmp[:], pos[:], oh[:, c], ALU.mult))
                    step(ve_.tensor_reduce(col(SL), tmp[:], AX.X, ALU.add))
                    step(ve_.tensor_scalar(col(VA), col(SL), float(CAP), float(SLOTS), ALU.is_ge, ALU.mult))
                    step(ve_.tensor_tensor(col(SL), col(SL), col(VA), ALU.add))
                    step(ve_.tensor_tensor(tmp[:], oh[:, c], ecap[:].unsqueeze(1).to_broadcast([P, NT, E]), ALU.mult))
                    step(ve_.tensor_reduce(col(VA), tmp[:], AX.X, ALU.add))
                    step(ve_.tensor_tensor(slot_i[:, c, :], col(SL), col(VA), ALU.add))
                    step(ve_.tensor_tensor(rec[:, c, :, 1], col(G1 + c), col(WS), ALU.mult))
                    ids = tok_id[:, bass.ds(b * NT, NT)]
                    carry(dve)
                    last = ve_.tensor_copy(rec[:, c, :, 0].bitcast(I32), ids)
                    if c == 0:
                        step(last)
                assert k[0] == ROUTE_STEPS, k[0]
                last.then_inc(rec_done, 1)

            with dve.Fori(0, B) as b:
                batch(b)

            k = [0]

            def planning(ins):
                k[0] += 1
                ins.then_inc(planned, 1)
                dve.wait_ge(planned, k[0])

            rows_of = base[:, NT, :]
            planning(ve_.memset(plan_f[:], 0.0))
            for j in range(1, TPE):
                planning(ve_.scalar_tensor_tensor(out=plan_f[:, EXTRA, 0:E], in0=rows_of, scalar=float(j * TT),
                                                  in1=plan_f[:, EXTRA, 0:E], op0=ALU.is_gt, op1=ALU.add))
            for e in range(E):
                planning(ve_.scalar_tensor_tensor(out=plan_f[:, BEFORE, e + 1:e + 2], in0=plan_f[:, BEFORE, e:e + 1],
                                                  scalar=1.0, in1=plan_f[:, EXTRA, e:e + 1], op0=ALU.add, op1=ALU.add))
            ve_.tensor_copy(plan[:], plan_f[:]).then_inc(plan_ready, 1)
            dve.wait_ge(plan_ready, 1)
            dve.drain().then_inc(phase_a, 1)

            def w1_lo_part(e, j):
                dve.wait_ge(w1_split_hi, PAIRS * e + j + 1)
                ve_.tensor_tensor(w1_lo[:, :, 256 * j:256 * (j + 1)],
                                  stage1[:, j % RING, :].rearrange("p (c h) -> p c h", c=KC),
                                  w1_hi[:, :, 256 * j:256 * (j + 1)].bitcast(F32), ALU.subtract).then_inc(w1_ready, 1)

            def w2_lo_part(e, j):
                dve.wait_ge(w2_split_hi, PAIRS * e + j + 1)
                ve_.tensor_tensor(w2_lo[:, 2 * j:2 * j + 2, :],
                                  stage2[:, j % RING, :].rearrange("p (c d) -> p c d", c=2),
                                  w2_hi[:, 2 * j:2 * j + 2, :].bitcast(F32), ALU.subtract).then_inc(w2_ready, 1)

            def rows_lo(g):
                for c in range(2):
                    dve.wait_ge(et_split_hi, 2 * g + c + 1)
                    ve_.tensor_tensor(et_lo[:, 2 * c:2 * c + 2, :], et_bank[c][:].rearrange("p (c t) -> p c t", c=2),
                                      et_hi[:, 2 * c:2 * c + 2, :].bitcast(F32), ALU.subtract).then_inc(et_ready, 1)

            def y_bias(e, g):
                dve.wait_ge(b2_landed, 16 * (e + 1))
                dve.wait_ge(adds_done, g + 1)
                for h in range(HT):
                    dve.wait_ge(mm2_done, MC * (g + 1) + 4)
                    ve_.tensor_tensor(ys[:, h, :], y_bank[h][:], b2_cur[:], ALU.add).then_inc(y_read, 1)

            def tile(e, g, final, more):
                for mm in range(MC):
                    v = MC * g + mm
                    dve.wait_ge(h32_done, v + 5)
                    dve.wait_ge(mm2_done, v + 1)
                    ve_.tensor_copy(h_hi[:, mm % 4, :], h32[:, mm % 2, :]).then_inc(h_split_hi, 1)
                    dve.wait_ge(h_split_hi, v + 1)
                    ve_.tensor_tensor(h_lo[:, mm % 4, :], h32[:, mm % 2, :], h_hi[:, mm % 4, :].bitcast(F32),
                                      ALU.subtract).then_inc(h_ready, 1)
                    if final and more and mm % 2 == 1:
                        j = mm // 2
                        w1_lo_part(e + 1, j)
                        if j >= 2:
                            w2_lo_part(e + 1, j - 2)
                if more or not final:
                    rows_lo(g + 1)
                if final and more:
                    w2_lo_part(e + 1, PAIRS - 2)
                y_bias(e, g)
                if final and more:
                    w2_lo_part(e + 1, PAIRS - 1)

            dve.wait_ge(phase_a, 4)
            for j in range(PAIRS):
                w1_lo_part(0, j)
                w2_lo_part(0, j)
            rows_lo(0)

            def expert(e, more):
                extra, before = tiles_of(dve, e)
                with dve.Fori(0, TPE - 1) as t:
                    with dve.If(t < extra):
                        tile(e, before + t, False, more)
                tile(e, before + extra, True, more)

            with dve.Fori(0, E - 1) as e:
                expert(e, True)
            expert(E - 1, False)

        @block.tensor
        def _(pe):
            mm_ = nc.tensor.matmul
            pe.sem_inc(kv_acc, 2)
            pe.sem_inc(o_full, 1)
            pe.sem_inc(lg_full, 1)
            pe.sem_inc(mm2_done, 4)
            pe.sem_inc(et_full, 1)
            pe.wait_ge(const_done, 3)
            pe.wait_ge(dconst_done, 2)

            def product(out_, left, right, n, first=True, last=True):
                for c in range(n):
                    lh, ll = left(c)
                    rh, rl = right(c)
                    mm_(out_, lh, rh, start=(first and c == 0), stop=False)
                    mm_(out_, lh, rl, start=False, stop=False)
                    ins = mm_(out_, ll, rh, start=False, stop=(last and c == n - 1))
                return ins

            def turn(dst, src):
                for c in range(KC):
                    ins = nc.tensor.transpose(dst[:, P * c:P * (c + 1)], src[:, P * c:P * (c + 1)], ident[:])
                return ins

            def batch(b):
                for s in range(STEPS):
                    i = s - 2
                    if 0 <= i < NT:
                        pe.wait_ge(xn_done, NT * b + i + 1)
                        pe.wait_ge(tr_lo, 2 * NT * b + i + 1)
                        turn(bank[0], xn[:, i % 2, :]).then_inc(tr_full, 1)
                    c = s - 6
                    if 0 <= c < HB * KC:
                        v = HB * KC * b + c
                        o, h = c % KC, c // KC
                        pe.wait_ge(st_lo, 3)
                        pe.wait_ge(tr_lo, 2 * NT * b + 4 * h + 5)
                        pe.wait_ge(qt_done, v + 1)
                        product(bank[3][:], lambda k: (whi["q"][:, k, P * o:P * (o + 1)], wlo["q"][:, k, P * o:P * (o + 1)]),
                                lambda k: (xt_hi[:, k, 512 * h:512 * (h + 1)], xt_lo[:, k, 512 * h:512 * (h + 1)]),
                                KC).then_inc(q_full, 1)
                    i = s - 3
                    if 0 <= i < NT:
                        v = NT * b + i
                        toks = lambda k: (xt_hi[:, k, P * i:P * (i + 1)], xt_lo[:, k, P * i:P * (i + 1)])
                        pe.wait_ge(st_lo, 2)
                        pe.wait_ge(tr_lo, 2 * NT * b + i + 2)
                        pe.wait_ge(kt_done, v + 1)
                        product(bank[1][:], toks, lambda k: (whi["k"][:, k, :], wlo["k"][:, k, :]), KC).then_inc(k_full, 1)
                        pe.wait_ge(v_done, v + 1)
                        product(bank[2][:], toks, lambda k: (whi["v"][:, k, :], wlo["v"][:, k, :]), KC).then_inc(v_full, 1)
                    i = s - 4
                    if 0 <= i < NT:
                        v = NT * b + i
                        pe.wait_ge(kp_done, v + 2)
                        pe.wait_ge(v_done, v + 2)
                        for g in range(G):
                            dst = bank[4 + g // 2][:, (P + 1) * (g % 2):(P + 1) * (g % 2 + 1)]
                            ins = mm_(dst, kp[:, i % 2, P * g:P * (g + 1)], vx[:, i % 2, g, :],
                                      start=(i == 0 and g % 2 == 0), stop=(i == NT - 1), skip_group_check=True)
                        ins.then_inc(kv_acc, 1)
                    i = s - T0
                    if 0 <= i < NT:
                        v = NT * b + i
                        pe.wait_ge(kvd_done, 2 * (b + 1))
                        pe.wait_ge(qp_done, HB * KC * b + KC * (i // 4 + 1) + 1)
                        pe.wait_ge(at_done, v + 1)
                        pe.wait_ge(z_read, v + 1)
                        for g in range(G):
                            q_ = qp[:, g, P * i:P * (i + 1)]
                            mm_(bank[4][:, HPG * g:HPG * (g + 1)], q_, ksd[:, g, :], start=True, stop=True)
                            ins = mm_(bank[6][:, P * g:P * (g + 1)], q_, kvd[:, g, :], start=True, stop=True)
                        ins.then_inc(num_full, 1)
                    i = s - T0 - 1
                    if 0 <= i < NT:
                        pe.wait_ge(at_done, NT * b + i + 2)
                        pe.wait_ge(tr_lo, 2 * NT * b + NT + i + 1)
                        turn(bank[0], at[:]).then_inc(tr_full, 1)
                    i = s - T0 - 4
                    if 0 <= i < NT:
                        v = NT * b + i
                        pe.wait_ge(x1n_done, v + 1)
                        if i > 0:
                            pe.wait_ge(nt_done, v)
                        turn(bank[7], x1n[:, i % 2, :]).then_inc(nt_full, 1)
                    i = s - T0 - 2
                    if 0 <= i < NT:
                        v = NT * b + i
                        pe.wait_ge(st_lo, 4)
                        pe.wait_ge(tr_lo, 2 * NT * b + NT + i + 2)
                        if i >= 2:
                            pe.wait_ge(x1_done, v - 1)
                        product(bank[1 + i % 2][:], lambda k: (at_hi[:, k, :], at_lo[:, k, :]),
                                lambda k: (whi["o"][:, k, :], wlo["o"][:, k, :]), KC).then_inc(o_full, 1)
                    i = s - T0 - 5
                    if 0 <= i < NT:
                        pe.wait_ge(nt_done, NT * b + i + 1)
                        for k in range(KC):
                            ins = mm_(bank[5][:, E * i:E * (i + 1)], nt[:, k, :], gw[:, k, :], start=(k == 0),
                                      stop=(k == KC - 1))
                        ins.then_inc(lg_full, 1)
                pe.wait_ge(cnt_done, b + 1)
                c2 = cnt[:].rearrange("p t e -> p (t e)")
                mm_(bank[5][:, R:2 * R], upper[:], c2, start=True, stop=True)
                mm_(bank[5][:, 2 * R:3 * R], ones[:], c2, start=True, stop=True).then_inc(cum_full, 1)

            with pe.Fori(0, B) as b:
                batch(b)
            pe.drain().then_inc(phase_a, 1)

            def rows(g):
                for h in range(HT):
                    pe.wait_ge(gathered[h], 16 * (g + 1))
                if not (isinstance(g, int) and g == 0):
                    pe.wait_ge(et_ready, 2 * g)
                for c in range(2):
                    for k in range(2):
                        for h in range(HT):
                            ins = nc.tensor.transpose(et_bank[c][:, TT * k + P * h:TT * k + P * (h + 1)],
                                                      xg[:, h, P * (2 * c + k):P * (2 * c + k + 1)], ident[:])
                    ins.then_inc(et_full, 1)

            def tile(e, g, more):
                for mm in range(MC + LAG):
                    if mm < MC:
                        if mm % 2 == 0:
                            pe.wait_ge(w1_ready, PAIRS * e + mm // 2 + 1 + RING)
                        pe.wait_ge(h32_done, MC * g + mm + 1)
                        if mm == 0:
                            pe.wait_ge(et_ready, 2 * g + 2)
                        cols = slice(P * mm, P * (mm + 1))
                        product(h_bank[mm % 4][:, 0:TT], lambda k: (w1_hi[:, k, cols], w1_lo[:, k, cols]),
                                lambda k: (et_hi[:, k, :], et_lo[:, k, :]), KC).then_inc(h_full, 1)
                    if mm == MC // 2 and more:
                        rows(g + 1)
                    n = mm - LAG
                    if n >= 0:
                        if n % 2 == 0:
                            pe.wait_ge(w2_ready, PAIRS * e + n // 2 + 1 + RING)
                        pe.wait_ge(h_ready, MC * g + n + 3)
                        if n == 0:
                            pe.wait_ge(y_read, HT * g + 1)
                        for h in range(HT):
                            toks = slice(P * h, P * (h + 1))
                            ins = product(y_bank[h][:], lambda k: (h_hi[:, n % 4, toks], h_lo[:, n % 4, toks]),
                                          lambda k: (w2_hi[:, n, :], w2_lo[:, n, :]), 1, first=(n == 0),
                                          last=(n == MC - 1))
                        ins.then_inc(mm2_done, 1)

            pe.wait_ge(phase_a, 4)
            rows(0)

            def expert(e, more):
                extra, before = tiles_of(pe, e)
                with pe.Fori(0, TPE - 1) as t:
                    with pe.If(t < extra):
                        tile(e, before + t, True)
                tile(e, before + extra, more)

            with pe.Fori(0, E - 1) as e:
                expert(e, True)
            expert(E - 1, False)


_INS = ["hidden_states", "q_w", "q_b", "k_w", "k_b", "v_w", "v_b", "o_w", "o_b"]
_FFN = ["gating_w", "w1", "b1", "w2", "b2"]


def kernel(**inputs):
    import numpy as _np
    import concourse.bacc as _bacc
    from concourse import mybir as _mybir
    from concourse.bass_utils import run_bass_kernel_spmd as _run

    nc = _bacc.Bacc("TRN2", target_bir_lowering=False, num_devices=1)
    arrays, args = {}, []
    for name in [f"L0_attn_{n}" for n in _INS] + [f"L0_ffn_{n}" for n in _FFN]:
        a = _np.asarray(inputs[name])
        if name in ("L0_attn_q_w", "L0_attn_k_w", "L0_attn_v_w", "L0_attn_o_w"):
            a = a.T
        a = _np.ascontiguousarray(a)
        arrays[f"{name}_dram"] = a
        args.append(nc.dram_tensor(f"{name}_dram", a.shape, _mybir.dt.from_np(a.dtype), kind="ExternalInput").ap())
    x = inputs["L0_attn_hidden_states"]
    b, s, d = x.shape
    out = nc.dram_tensor("out_dram", (b * s + PAD, d), _mybir.dt.float32, kind="ExternalOutput").ap()
    moe_block(nc, *args, out)
    r = _run(nc, [arrays], core_ids=[0])
    return r.results[0]["out_dram"][0:b * s].reshape(b, s, d)
```

```python
from contextlib import ExitStack

import concourse.bass as bass
from concourse import mybir

F32 = mybir.dt.float32
F32R = mybir.dt.float32r
I32 = mybir.dt.int32
ALU = mybir.AluOpType
ACT = mybir.ActivationFunctionType
AX = mybir.AxisListType

P = 128
HEAD_DIM = 32
LN_EPS = 1e-5
Z_EPS = 1e-6
W_EPS = 1e-8
CAPACITY_NUM, CAPACITY_DEN = 5, 4
TOP_K = 2
PAD = 256


def moe_block(nc, x_in, wq_t, bq, wk_t, bk, wv_t, bv, wo_t, bo, gate_w, w1, b1, w2, b2, out):
    B, S, D = x_in.shape
    E, _, HID = w1.shape
    T = B * S
    NT = S // P
    KC = D // P
    G = KC
    HPG = P // HEAD_DIM
    CAP = T * TOP_K * CAPACITY_NUM // (E * CAPACITY_DEN)
    SLOTS = E * CAP
    TT = 256
    HT = TT // P
    TPE = CAP // TT
    MC = HID // P
    PAIRS = MC // 2
    HB = S // 512
    R = NT * E
    ROUTE_STEPS = 37 + NT
    RING = 4
    assert CAP % TT == 0 and E * TPE < 64 and D == 512 and HB == 2 and NT == 8

    xrows = x_in.rearrange("b (t p) d -> b t p d", p=P)
    out_t = out[0:T, :].rearrange("(b t p) d -> b t p d", b=B, p=P)
    normed = nc.dram_tensor("normed", [T + PAD, D], F32).ap()
    normed_t = normed[0:T, :].rearrange("(b t p) d -> b t p d", b=B, p=P)
    table = nc.dram_tensor("slot_table", [SLOTS + TT, 2], F32).ap()
    table_t = table.rearrange("(g h p) c -> g p h c", h=HT, p=P)

    ctx = ExitStack()
    with ctx:
        def sb(name, shape, dt=F32, scope=ctx):
            return scope.enter_context(nc.sbuf_tensor(name, shape, dt))

        def sem(name):
            return ctx.enter_context(nc.semaphore(name))

        bank = [ctx.enter_context(nc.psum_tensor(f"bank{i}", [P, 512], F32)) for i in range(8)]

        stage = sb("stage", [P, 2, 2048])
        ident = sb("ident", [P, P])
        plan_f = sb("plan_f", [P, 3, E + 1])
        plan = sb("plan", [P, E], I32)
        EXTRA, BEFORE, BOTH = range(3)
        b1_all = sb("b1_all", [P, E, MC])

        pa = ExitStack()
        sa = lambda name, shape, dt=F32: sb(name, shape, dt, pa)
        whi, wlo = {}, {}
        for c in "kvq":
            whi[c], wlo[c] = sa(f"w{c}_hi", [P, KC, D], F32R), sa(f"w{c}_lo", [P, KC, D], F32R)
        xt_hi = sa("xt_hi", [P, KC, S], F32R)
        xt_lo = sa("xt_lo", [P, KC, S], F32R)
        whi["o"], wlo["o"] = sa("wo_hi", [P, KC, D], F32R), sa("wo_lo", [P, KC, D], F32R)
        xb = sa("xb", [P, NT, D])
        qp = sa("qp", [P, KC, S])
        xn = sa("xn", [P, 2, D])
        kt = sa("kt", [P, D])
        ke = sa("ke", [P, D])
        kp = sa("kp", [P, 2, D])
        vx = sa("vx", [P, 2, G, P + 1])
        qt = sa("qt", [P, 512])
        qe = sa("qe", [P, 512])
        bkb = sa("bkb", [P, D])
        bvb = sa("bvb", [P, D])
        bob = sa("bob", [P, D])
        bqt = sa("bqt", [P, KC])
        kvd = sa("kvd", [P, G, P + HPG])
        at = sa("at", [P, 2, D])
        at_hi = sa("at_hi", [P, 2, KC, P], F32R)
        at_lo = sa("at_lo", [P, 2, KC, P], F32R)
        x1 = sa("x1", [P, 2, D])
        x1n = sa("x1n", [P, 2, D])
        nt = sa("nt", [P, KC, P])
        gw = sa("gw", [P, KC, E])
        stats = sa("stats", [P, 2, 6])
        mv = sa("mv", [P, 2, 2])
        ve = sa("ve", [P, 2])
        rstd = sa("rstd", [P, 2])
        stats2 = sa("stats2", [P, 6])
        mv2 = sa("mv2", [P, 2])
        ve2 = sa("ve2", [P, 1])
        rstd2 = sa("rstd2", [P, 1])
        nhalf = sa("nhalf", [P, 1])
        zi = sa("zi", [P, 2, G, HPG])
        headmask = sa("headmask", [P, HPG, HEAD_DIM])
        upper = sa("upper", [P, P])
        ones = sa("ones", [P, P])
        zrow = sa("zrow", [P, D])
        tabinit_i = sa("tabinit_i", [P, SLOTS // P], I32)
        tabinit = sa("tabinit", [P, SLOTS // P, 2])
        tok_id = sa("tok_id", [P, T // P], I32)
        ei = sa("ei", [P, E], I32)
        ef = sa("ef", [P, E])
        ecap = sa("ecap", [P, E])
        lg = sa("lg", [P, NT, E])
        gt = sa("gt", [P, NT, E])
        tmp = sa("tmp", [P, NT, E])
        oh = sa("oh", [P, 2, NT, E])
        cnt = sa("cnt", [P, NT, E])
        pos = sa("pos", [P, NT, E])
        cums = sa("cums", [P, 2, R])
        base = sa("base", [P, NT + 1, E])
        m = sa("m", [P, 8, NT])
        slot_i = sa("slot_i", [P, 2, NT], I32)
        rec = sa("rec", [P, 2, NT, 2])
        RM, RS, G1, G2, I1, WS, VA, SL = range(8)

        n_ = sem
        x_landed = [n_(f"x_landed{i}") for i in range(NT)]
        st_landed = [n_(f"st_landed{i}") for i in range(2)]
        small_landed = n_("small_landed")
        const_done, const_set, mask_cut = n_("const_done"), n_("const_set"), n_("mask_cut")
        dconst_done, tab_zeroed, base_zeroed = n_("dconst_done"), n_("tab_zeroed"), n_("base_zeroed")
        zrow_stored = n_("zrow_stored")
        tab_stored = n_("tab_stored")
        st_hi, st_lo = n_("st_hi"), n_("st_lo")
        stats_done, mv_done, ve_done, rstd_done = n_("stats_done"), n_("mv_done"), n_("ve_done"), n_("rstd_done")
        xn_done, bo_added = n_("xn_done"), n_("bo_added")
        xt_full, xt_hi_done, xt_lo_done = n_("xt_full"), n_("xt_hi_done"), n_("xt_lo_done")
        att_full, att_hi_done, att_lo_done = n_("att_full"), n_("att_hi_done"), n_("att_lo_done")
        k_full, kt_done, km_done, ke_done, kp_done = n_("k_full"), n_("kt_done"), n_("km_done"), n_("ke_done"), n_("kp_done")
        v_full, v_done = n_("v_full"), n_("v_done")
        kv_acc = n_("kv_acc")
        kvd_done = n_("kvd_done")
        q_full, qt_done, qm_done, qe_done, qp_done = n_("q_full"), n_("qt_done"), n_("qm_done"), n_("qe_done"), n_("qp_done")
        num_full, z_read, z_rec, at_done = n_("num_full"), n_("z_read"), n_("z_rec"), n_("at_done")
        o_full, x1_done = n_("o_full"), n_("x1_done")
        x1_stored = [n_(f"x1_stored{i}") for i in range(2)]
        stats2_done, mv2_done, ve2_done = n_("stats2_done"), n_("mv2_done"), n_("ve2_done")
        rstd2_done, x1n_done = n_("rstd2_done"), n_("x1n_done")
        x1n_stored = [n_(f"x1n_stored{i}") for i in range(2)]
        nt_full, nt_done = n_("nt_full"), n_("nt_done")
        lg_full = n_("lg_full")
        route = n_("route")
        lg_exp_in, lg_exp = n_("lg_exp_in"), n_("lg_exp")
        cnt_done, cum_full = n_("cnt_done"), n_("cum_full")
        cum_read, rec_done = n_("cum_read"), n_("rec_done")
        ids_done = n_("ids_done")
        scattered = [n_(f"scattered{i}") for i in range(4)]
        recs_free = n_("recs_free")
        phase_a = n_("phase_a")

        pb = ExitStack()

        LEAD = 4
        STEPS = LEAD + NT + 6
        W1_STEPS = [j if j < RING else j + 1 for j in range(PAIRS)]
        W = P + HPG
        Z0 = 3 * R
        QC = HB * KC
        N_ATT = B * QC

        MATRICES = "vkqo"
        MATRIX_STEPS = (LEAD + 2, LEAD + 2, LEAD + 5, LEAD + 7)

        def due(batch_, i, count=NT):
            return batch_ is not None and 0 <= i < count

        carrier = n_("carrier")
        planned, plan_ready = n_("planned"), n_("plan_ready")

        def carry(eng):
            eng.sem_inc(carrier, 1)

        def tiles_of(eng, e):
            n = eng.value_load(plan[0:1, slice(e, e + 1) if isinstance(e, int) else bass.ds(e, 1)],
                               min_val=0, max_val=128 * TPE - 1)
            return n >> 7, (n & 127) >> 1, n & 1

        def staged(eng, n):
            eng.wait_ge(st_landed[n % 2], 16 * (n // 2 + 1))

        def alloc_b():
            names = {}
            b = lambda name, shape, dt=F32: names.__setitem__(name, sb(name, shape, dt, pb))
            b("w1_hi", [P, KC, HID], F32R)
            b("w1_lo", [P, KC, HID], F32R)
            b("stage2", [P, RING, 1024])
            b("w2_hi", [P, MC, D], F32R)
            b("w2_lo", [P, MC, D], F32R)
            b("xg", [P, HT, D])
            b("et_hi", [P, KC, TT], F32R)
            b("et_lo", [P, KC, TT], F32R)
            b("h32", [P, 2, TT])
            b("h_hi", [P, 4, TT], F32R)
            b("h_lo", [P, 4, TT], F32R)
            b("ys", [P, HT, D])
            b("b1_cur", [P, MC])
            b("b2_cur", [P, D])
            b("tab_g", [P, HT, 2])
            b("tab_s", [P, HT, 2])
            return names

        pa.close()
        nb = alloc_b()
        w1_hi, w1_lo, w2_hi, w2_lo = (nb[k] for k in ("w1_hi", "w1_lo", "w2_hi", "w2_lo"))
        stage2 = nb["stage2"]
        stage1 = stage[:].rearrange("p a (b c) -> p (a b) c", c=1024)
        xg, et_hi, et_lo, h32, h_hi, h_lo = (nb[k] for k in ("xg", "et_hi", "et_lo", "h32", "h_hi", "h_lo"))
        ys, b1_cur, b2_cur, tab_g, tab_s = (nb[k] for k in ("ys", "b1_cur", "b2_cur", "tab_g", "tab_s"))
        w1_landed = [n_(f"w1_landed{i}") for i in range(RING)]
        w2_landed = [n_(f"w2_landed{i}") for i in range(RING)]
        w1_split_hi, w1_ready = n_("w1_split_hi"), n_("w1_ready")
        w2_split_hi, w2_ready = n_("w2_split_hi"), n_("w2_ready")
        b1_landed, b1_copied = n_("b1_landed"), n_("b1_copied")
        b2_landed = n_("b2_landed")
        tabg_landed, tabs_landed = n_("tabg_landed"), n_("tabs_landed")
        gathered = [n_(f"gathered{i}") for i in range(HT)]
        added = [n_(f"added{i}") for i in range(HT)]
        adds_done = n_("adds_done")
        et_full, et_split_hi, et_ready = n_("et_full"), n_("et_split_hi"), n_("et_ready")
        h_full, h32_done, h_split_hi, h_ready = n_("h_full"), n_("h32_done"), n_("h_split_hi"), n_("h_ready")
        mm2_done = n_("mm2_done")
        y_read, y_done, y_cleared = n_("y_read"), n_("y_done"), n_("y_cleared")
        ctx.enter_context(pb)

        h_bank = bank[0:4]
        et_bank = bank[4:6]
        y_bank = bank[6:8]
        LAG = 3

        block = ctx.enter_context(nc.Block())

        @block.sync
        def _(sp):
            def load_x(b, i):
                sp.dma_start(xb[:, i, :], xrows[b, i] if isinstance(b, int) else
                             xrows[bass.ds(b, 1), i].rearrange("a p d -> (a p) d")).then_inc(x_landed[i], 16)

            for i in range(2):
                sp.sem_inc(x1_stored[i], 16)
                sp.sem_inc(x1n_stored[i], 16)
            def load_matrix(m, w):
                if m >= 2:
                    sp.wait_ge(st_lo, m - 1)
                sp.dma_start(stage[:, m % 2, :].rearrange("p (c d) -> p c d", c=KC),
                             w.rearrange("(c p) d -> p c d", p=P)).then_inc(st_landed[m % 2], 16)

            load_x(0, 0)
            load_x(0, 1)
            load_matrix(0, wv_t)
            load_x(0, 2)
            load_matrix(1, wk_t)
            sp.dma_start(bkb[:], bk.partition_broadcast(P)).then_inc(small_landed, 16)
            sp.dma_start(bvb[:], bv.partition_broadcast(P)).then_inc(small_landed, 16)
            sp.dma_start(bob[:], bo.partition_broadcast(P)).then_inc(small_landed, 16)
            sp.dma_start(gw[:], gate_w.rearrange("(c p) e -> p c e", p=P)).then_inc(small_landed, 16)
            with nc.allow_non_contiguous_dma(reason="512 biases"):
                sp.dma_start(bqt[:], bq.rearrange("(c p) -> p c", p=P)).then_inc(small_landed, 16)
            load_x(0, 3)
            load_matrix(2, wq_t)
            for i in range(4, NT):
                load_x(0, i)
            load_matrix(3, wo_t)
            with nc.allow_non_contiguous_dma(reason="biases laid out by partition"):
                sp.dma_start(b1_all[:], b1.rearrange("e (c p) -> p e c", p=P)).then_inc(b1_landed, 16)
            sp.wait_ge(dconst_done, 2)
            for r in range(PAD // P):
                sp.dma_start(normed[T + r * P:T + (r + 1) * P, :], zrow[:]).then_inc(zrow_stored, 16)
                sp.dma_start(out[T + r * P:T + (r + 1) * P, :], zrow[:]).then_inc(zrow_stored, 16)
            sp.dma_start(table[0:SLOTS, :].rearrange("(p s) c -> p s c", p=P), tabinit[:]).then_inc(tab_stored, 16)

            def load_w1(e, j):
                sp.wait_ge(w1_ready, PAIRS * e + j + 1)
                w1v = w1[e] if isinstance(e, int) else w1[bass.ds(e, 1)].rearrange("a d h -> (a d) h")
                sp.dma_start(stage1[:, j % RING, :].rearrange("p (c h) -> p c h", c=KC),
                             w1v[:, 256 * j:256 * (j + 1)].rearrange("(c p) h -> p c h", p=P)) \
                    .then_inc(w1_landed[j % RING], 16)

            def load_w2(e, j):
                sp.wait_ge(w2_ready, PAIRS * e + j + 1)
                w2v = w2[e] if isinstance(e, int) else w2[bass.ds(e, 1)].rearrange("a h d -> (a h) d")
                sp.dma_start(stage2[:, j % RING, :].rearrange("p (c d) -> p c d", c=2),
                             w2v[256 * j:256 * (j + 1), :].rearrange("(c p) d -> p c d", p=P)) \
                    .then_inc(w2_landed[j % RING], 16)

            def batch(b, last):
                for i in range(NT):
                    v = NT * b + i
                    sp.wait_ge(x1_done, v + 1)
                    sp.dma_start(out_t[bass.ds(b, 1), i].rearrange("a p d -> (a p) d"), x1[:, i % 2, :]) \
                        .then_inc(x1_stored[i % 2], 16)
                    if last and i < RING:
                        load_w1(0, RING + i)
                    elif last:
                        if i == RING:
                            sp.wait_ge(q_full, N_ATT)
                        load_w2(0, i - RING)
                    else:
                        sp.dma_start(xb[:, i, :], xrows[bass.ds(b + 1, 1), i].rearrange("a p d -> (a p) d")) \
                            .then_inc(x_landed[i], 16)
                    sp.wait_ge(x1n_done, v + 1)
                    sp.dma_start(normed_t[bass.ds(b, 1), i].rearrange("a p d -> (a p) d"), x1n[:, i % 2, :]) \
                        .then_inc(x1n_stored[i % 2], 16)

            sp.wait_ge(st_lo, 4)
            for j in range(RING):
                load_w1(0, j)
            with sp.Fori(0, B - 1) as b:
                batch(b, False)
            batch(B - 1, True)
            for j in range(RING, PAIRS):
                load_w2(0, j)
            for i in range(2):
                sp.wait_ge(x1_stored[i], 16 * (T // P // 2 + 1))
                sp.wait_ge(x1n_stored[i], 16 * (T // P // 2 + 1))

            def load_tab_g(g):
                sp.dma_start(tab_g[:], table_t[bass.ds(g, 1)].rearrange("a p h c -> (a p) h c")
                             if not isinstance(g, int) else table_t[g]).then_inc(tabg_landed, 16)

            def load_tab_s(g):
                sp.dma_start(tab_s[:], table_t[bass.ds(g, 1)].rearrange("a p h c -> (a p) h c")
                             if not isinstance(g, int) else table_t[g]).then_inc(tabs_landed, 16)

            sp.wait_ge(phase_a, 4)
            load_tab_g(0)
            for h in range(HT):
                sp.wait_ge(gathered[h], 16)

            def gather_records(e, before, extra, t, more):
                for h in range(HT):
                    sp.wait_ge(gathered[h], 16 * (before + t + 1))
                carry(sp)
                with sp.If(t < extra) if not isinstance(t, int) else sp.If(extra > t):
                    load_tab_g(e * TPE + t + 1)
                if more:
                    with sp.If(extra < t + 1):
                        load_tab_g((e + 1) * TPE)

            def add_records(e, before, t):
                sp.wait_ge(adds_done, before + t + 1)
                load_tab_s(e * TPE + t)

            def load_b2(e, before):
                sp.wait_ge(y_read, HT * before + 1)
                b2v = b2[e:e + 1, :] if isinstance(e, int) else b2[bass.ds(e, 1), :]
                sp.dma_start(b2_cur[:], b2v.rearrange("a d -> (a d)").partition_broadcast(P)).then_inc(b2_landed, 16)

            def expert(e, more):
                extra, before, _ = tiles_of(sp, e)
                gather_records(e, before, extra, 0, more)
                load_b2(e, before)
                add_records(e, before, 0)
                if more:
                    for h in range(HT):
                        sp.wait_ge(gathered[h], 16 * (before + 2))
                    carry(sp)
                    for j in range(RING):
                        load_w1(e + 1, j)
                        load_w2(e + 1, j)
                with sp.Fori(1, TPE) as t:
                    with sp.If(t < extra + 1):
                        gather_records(e, before, extra, t, more)
                        add_records(e, before, t)
                if more:
                    for j in range(RING, PAIRS + 2):
                        if j < PAIRS:
                            load_w1(e + 1, j)
                        if j >= RING + 2:
                            load_w2(e + 1, j - 2)

            with sp.Fori(0, E - 1) as e:
                expert(e, True)
            expert(E - 1, False)

        @block.gpsimd
        def _(pool):
            nc.gpsimd.memset(ident[:], 0.0).then_inc(const_set, 1)
            nc.gpsimd.memset(headmask[:], 1.0).then_inc(const_set, 1)
            nc.gpsimd.memset(upper[:], 1.0).then_inc(const_set, 1)
            nc.gpsimd.memset(nhalf[:], -0.5).then_inc(const_set, 1)
            nc.gpsimd.iota(tabinit_i[:], [[1, SLOTS // P]], base=0, channel_multiplier=SLOTS // P).then_inc(ids_done, 1)
            nc.gpsimd.iota(tok_id[:], [[P, T // P]], base=0, channel_multiplier=1).then_inc(ids_done, 1)
            nc.gpsimd.iota(ei[:], [[1, E]], base=0, channel_multiplier=0).then_inc(ids_done, 1)
            pool.wait_ge(const_set, 4)
            nc.gpsimd.affine_select(out=ident[:], in_=ident[:], compare_op=ALU.not_equal, fill=1.0, base=0,
                                    pattern=[[-1, P]], channel_multiplier=1).then_inc(const_done, 1)
            nc.gpsimd.affine_select(out=headmask[:], in_=headmask[:], compare_op=ALU.is_ge, fill=0.0, base=0,
                                    pattern=[[-HEAD_DIM, HPG], [0, HEAD_DIM]], channel_multiplier=1).then_inc(mask_cut, 1)
            nc.gpsimd.affine_select(out=upper[:], in_=upper[:], compare_op=ALU.is_ge, fill=0.0, base=-1,
                                    pattern=[[1, P]], channel_multiplier=-1).then_inc(const_done, 1)
            pool.wait_ge(mask_cut, 1)
            nc.gpsimd.affine_select(out=headmask[:], in_=headmask[:], compare_op=ALU.is_ge, fill=0.0,
                                    base=HEAD_DIM - 1, pattern=[[HEAD_DIM, HPG], [0, HEAD_DIM]],
                                    channel_multiplier=-1).then_inc(const_done, 1)

            def norm_scale(v, done, var, tmp_, out_, step_done, ready):
                pool.wait_ge(done, v + 1)
                carry(pool)
                nc.gpsimd.tensor_scalar(tmp_, var, LN_EPS, None, ALU.add).then_inc(step_done, 1)
                pool.wait_ge(step_done, v + 1)
                nc.gpsimd.tensor_tensor(out_, tmp_, nhalf[:], ALU.pow).then_inc(ready, 1)

            def steps(a, n, first=0):
                for s in range(first, STEPS):
                    i = s - LEAD
                    if due(a, i):
                        norm_scale(NT * a + i, mv_done, mv[:, i % 2, 1:2], ve[:, i % 2:i % 2 + 1],
                                   rstd[:, i % 2:i % 2 + 1], ve_done, rstd_done)
                    i = s - LEAD - 1
                    if due(a, i):
                        if n is None and i == 0:
                            pool.wait_ge(small_landed, 80)
                        pool.wait_ge(xn_done, NT * a + i + 1)
                        nc.gpsimd.tensor_tensor(xb[:, i, :], xb[:, i, :], bob[:], ALU.add).then_inc(bo_added, 1)
                    i = s - 2
                    if due(n, i):
                        norm_scale(NT * n + i, mv2_done, mv2[:, 1:2], ve2[:], rstd2[:], ve2_done, rstd2_done)
                if n is not None:
                    scatter(n)

            def scatter(b):
                for c in range(TOP_K):
                    pool.wait_ge(rec_done, TOP_K * b + c + 1)
                    carry(pool)
                    for i in range(NT):
                        nc.gpsimd.indirect_dma_start(
                            out=table, out_offset=bass.IndirectOffsetOnAxis(ap=slot_i[:, c, i:i + 1], axis=0),
                            in_=rec[:, c, i, :], in_offset=None, bounds_check=SLOTS - 1, oob_is_err=False,
                        ).then_inc(scattered[(NT * c + i) % 4], 16)
                for q in range(4):
                    pool.wait_ge(scattered[q], 16 * (TOP_K * NT // 4) * (b + 1))
                pool.sem_inc(recs_free, 1)

            pool.sem_inc(recs_free, 1)
            steps(0, None, LEAD)
            pool.wait_ge(tab_stored, 16)
            with pool.Fori(0, B - 1) as b:
                steps(b + 1, b)
            steps(None, B - 1)
            pool.wait_ge(zrow_stored, 64)
            for i in range(2):
                pool.wait_ge(x1n_stored[i], 16 * (T // P // 2 + 1))
                pool.wait_ge(x1_stored[i], 16 * (T // P // 2 + 1))
            pool.drain().then_inc(phase_a, 1)

            def gather(g):
                pool.wait_ge(tabg_landed, 16 * (g + 1))
                pool.wait_ge(et_full, HT * g + 1)
                carry(pool)
                for h in range(HT):
                    nc.gpsimd.indirect_dma_start(
                        out=xg[:, h, :], out_offset=None, in_=normed,
                        in_offset=bass.IndirectOffsetOnAxis(ap=tab_g[:, h, 0:1].bitcast(I32), axis=0),
                    ).then_inc(gathered[h], 16)

            def add_rows(g):
                pool.wait_ge(y_done, HT * (g + 1))
                carry(pool)
                for h in range(HT):
                    nc.gpsimd.indirect_dma_start(
                        out=out, out_offset=bass.IndirectOffsetOnAxis(ap=tab_s[:, h, 0:1].bitcast(I32), axis=0),
                        in_=ys[:, h, :], in_offset=None, compute_op=ALU.add,
                    ).then_inc(added[h], 16)
                for h in range(HT):
                    pool.wait_ge(added[h], 16 * (g + 1))
                pool.sem_inc(adds_done, 1)

            pool.wait_ge(phase_a, 4)
            pool.sem_inc(adds_done, 1)
            gather(0)

            def expert(e, more):
                extra, before, _ = tiles_of(pool, e)
                with pool.Fori(0, TPE - 1) as t:
                    with pool.If(t < extra):
                        gather(before + t + 1)
                        add_rows(before + t)
                if more:
                    gather(before + extra + 1)
                add_rows(before + extra)

            with pool.Fori(0, E - 1) as e:
                expert(e, True)
            expert(E - 1, False)

        @block.scalar
        def _(act):
            def matrix_hi(m):
                staged(act, m)
                nc.scalar.activation(whi[MATRICES[m]][:], stage[:, m % 2, :].rearrange("p (c d) -> p c d", c=KC),
                                     ACT.Copy).then_inc(st_hi, 1)

            act.sem_inc(qt_done, 1)
            act.sem_inc(h32_done, 4)

            def split_hi(src, dst, done):
                nc.scalar.activation(dst, src[:].rearrange("p (c t) -> p c t", c=KC), ACT.Copy).then_inc(done, 1)

            def w1_split(e, j):
                act.wait_ge(w1_landed[j % RING], e * (16 * PAIRS // RING) + 16 * (j // RING + 1))
                nc.scalar.activation(w1_hi[:, :, 256 * j:256 * (j + 1)],
                                     stage1[:, j % RING, :].rearrange("p (c h) -> p c h", c=KC), ACT.Copy) \
                    .then_inc(w1_split_hi, 1)

            def w2_split(e, j):
                act.wait_ge(w2_landed[j % RING], e * (16 * PAIRS // RING) + 16 * (j // RING + 1))
                nc.scalar.activation(w2_hi[:, 2 * j:2 * j + 2, :],
                                     stage2[:, j % RING, :].rearrange("p (c d) -> p c d", c=2), ACT.Copy) \
                    .then_inc(w2_split_hi, 1)

            def steps(a, n, first=0):
                for s in range(first, STEPS):
                    i = s - LEAD - 2
                    if due(a, i):
                        act.wait_ge(xt_full, NT * a + i + 1)
                        split_hi(bank[0], xt_hi[:, :, P * i:P * (i + 1)], xt_hi_done)
                    for m_ in range(KC):
                        if n is None and s == MATRIX_STEPS[m_]:
                            matrix_hi(m_)
                    if n is None and s == LEAD + 2:
                        act.wait_ge(small_landed, 80)
                    c = s - LEAD - 6
                    if due(a, c, QC):
                        v = QC * a + c
                        act.wait_ge(q_full, v + 1)
                        act.wait_ge(qp_done, v + 1)
                        nc.scalar.activation(qt[:], bank[1][:], ACT.Identity, bias=bqt[:, c % KC:c % KC + 1]) \
                            .then_inc(qt_done, 1)
                        act.wait_ge(qm_done, v + 1)
                        nc.scalar.activation(qe[:], qe[:], ACT.Exp).then_inc(qe_done, 1)
                    i = s - 1
                    if due(n, i):
                        v = NT * n + i
                        if i >= 2:
                            act.wait_ge(o_full, v - 1)
                        act.wait_ge(att_full, v + 1)
                        split_hi(bank[7], at_hi[:, i % 2], att_hi_done)
                    i = s - LEAD - 3
                    if due(a, i):
                        act.wait_ge(km_done, NT * a + i + 1)
                        nc.scalar.activation(ke[:], ke[:], ACT.Exp).then_inc(ke_done, 1)
                    i = s - 3
                    if due(n, i):
                        v = NT * n + i
                        act.wait_ge(nt_full, v + 1)
                        act.wait_ge(lg_full, v + 1)
                        nc.scalar.activation(nt[:], bank[0][:].rearrange("p (c t) -> p c t", c=KC), ACT.Copy) \
                            .then_inc(nt_done, 1)
                    if n is not None and s == NT + 3:
                        act.wait_ge(lg_exp_in, n + 1)
                        nc.scalar.activation(gt[:], gt[:], ACT.Exp).then_inc(lg_exp, 1)
                    if a is None and s in W1_STEPS:
                        if s == W1_STEPS[0]:
                            act.wait_ge(q_full, N_ATT)
                        w1_split(0, W1_STEPS.index(s))

            steps(0, None, LEAD)
            with act.Fori(0, B - 1) as b:
                steps(b + 1, b)
            steps(None, B - 1)
            act.wait_ge(x1_done, T // P)
            for j in range(PAIRS):
                w2_split(0, j)
            act.drain().then_inc(phase_a, 1)

            def w2_used(g, j):
                act.wait_ge(mm2_done, MC * g + 2 * j + 2 + 4)

            def rows_hi(g):
                if not (isinstance(g, int) and g == 0):
                    act.wait_ge(h_full, MC * g)
                for c in range(2):
                    act.wait_ge(et_full, 2 * g + c + 2)
                    nc.scalar.activation(et_hi[:, 2 * c:2 * c + 2, :], et_bank[c][:].rearrange("p (c t) -> p c t", c=2),
                                         ACT.Copy).then_inc(et_split_hi, 1)

            def y_weight(g):
                act.wait_ge(tabs_landed, 16 * (g + 1))
                for h in range(HT):
                    act.wait_ge(y_read, HT * g + h + 2)
                    nc.scalar.activation(ys[:, h, :], ys[:, h, :], ACT.Copy, scale=tab_s[:, h, 1:2]) \
                        .then_inc(y_done, 1)

            def b1_load(e, before):
                src = b1_all[:, e, :] if isinstance(e, int) else b1_all[:, bass.ds(e, 1), :].rearrange("p a c -> p (a c)")
                act.wait_ge(h32_done, MC * before + 4)
                carry(act)
                nc.scalar.activation(b1_cur[:], src, ACT.Copy).then_inc(b1_copied, 1)
                act.wait_ge(b1_copied, e + 1)
                carry(act)

            def tile(e, g, final, more):
                for mm in range(MC):
                    v = MC * g + mm
                    act.wait_ge(h_full, v + 1)
                    act.wait_ge(h_ready, v + 1)
                    nc.scalar.activation(h32[:, mm % 2, :], h_bank[mm % 4][:, 0:TT], ACT.Relu,
                                         bias=b1_cur[:, mm:mm + 1]).then_inc(h32_done, 1)
                    if final and more and mm % 2 == 1:
                        w1_split(e + 1, mm // 2)
                    if final and more and mm % 2 == 0 and mm >= 4:
                        w2_used(g, mm // 2 - 2)
                        w2_split(e + 1, mm // 2 - 2)
                if more or not final:
                    rows_hi(g + 1)
                if final and more:
                    b1_load(e + 1, g + 1)
                    w2_used(g, PAIRS - 2)
                    w2_split(e + 1, PAIRS - 2)
                    w2_used(g, PAIRS - 1)
                    w2_split(e + 1, PAIRS - 1)
                y_weight(g)

            act.wait_ge(phase_a, 4)
            act.wait_ge(b1_landed, 16)
            b1_load(0, 0)
            rows_hi(0)

            def expert(e, more):
                extra, before, _ = tiles_of(act, e)
                with act.Fori(0, TPE - 1) as t:
                    with act.If(t < extra):
                        tile(e, before + t, False, more)
                tile(e, before + extra, True, more)

            with act.Fori(0, E - 1) as e:
                expert(e, True)
            expert(E - 1, False)

        @block.vector
        def _(dve):
            ve_ = nc.vector
            dve.sem_inc(qp_done, 1)
            dve.sem_inc(xt_lo_done, 1)
            dve.sem_inc(cum_read, 1)
            dve.sem_inc(z_rec, 1)
            dve.sem_inc(at_done, 1)
            dve.sem_inc(kt_done, 1)
            dve.sem_inc(kp_done, 1)
            dve.sem_inc(v_done, 1)
            dve.sem_inc(w1_ready, RING)
            dve.sem_inc(w2_ready, RING)
            dve.sem_inc(h_ready, 2)
            dve.sem_inc(y_read, 1)
            ve_.memset(ones[:], 1.0)
            ve_.memset(zrow[:], 0.0).then_inc(dconst_done, 1)
            ve_.memset(tabinit[:], 0.0).then_inc(tab_zeroed, 1)
            ve_.memset(vx[:, :, :, P:P + 1], 1.0)
            ve_.memset(base[:, NT, :], 0.0).then_inc(base_zeroed, 1)
            dve.wait_ge(base_zeroed, 1)
            dve.wait_ge(ids_done, 3)
            dve.wait_ge(tab_zeroed, 1)
            ve_.tensor_scalar(tabinit[:, :, 0].bitcast(I32), tabinit_i[:], PAD - 1, T, ALU.bitwise_and, ALU.bitwise_or) \
                .then_inc(dconst_done, 1)
            ve_.tensor_copy(ef[:], ei[:]).then_inc(ids_done, 1)
            dve.wait_ge(ids_done, 4)
            ve_.tensor_scalar(ecap[:], ef[:], float(CAP), None, ALU.mult).then_inc(ids_done, 1)
            dve.wait_ge(ids_done, 5)
            dve.wait_ge(const_done, 3)

            def matrix_lo(m):
                dve.wait_ge(st_hi, m + 1)
                ve_.tensor_tensor(wlo[MATRICES[m]][:], stage[:, m % 2, :].rearrange("p (c d) -> p c d", c=KC),
                                  whi[MATRICES[m]][:].bitcast(F32), ALU.subtract).then_inc(st_lo, 1)

            def split_lo(src, dst, hi, done):
                ve_.tensor_tensor(dst, src[:].rearrange("p (c t) -> p c t", c=KC), hi.bitcast(F32),
                                  ALU.subtract).then_inc(done, 1)

            def w1_lo_part(e, j):
                dve.wait_ge(w1_split_hi, PAIRS * e + j + 1)
                ve_.tensor_tensor(w1_lo[:, :, 256 * j:256 * (j + 1)],
                                  stage1[:, j % RING, :].rearrange("p (c h) -> p c h", c=KC),
                                  w1_hi[:, :, 256 * j:256 * (j + 1)].bitcast(F32), ALU.subtract).then_inc(w1_ready, 1)

            def w2_lo_part(e, j):
                dve.wait_ge(w2_split_hi, PAIRS * e + j + 1)
                ve_.tensor_tensor(w2_lo[:, 2 * j:2 * j + 2, :],
                                  stage2[:, j % RING, :].rearrange("p (c d) -> p c d", c=2),
                                  w2_hi[:, 2 * j:2 * j + 2, :].bitcast(F32), ALU.subtract).then_inc(w2_ready, 1)

            def steps(a, n, first=0):
                for s in range(first, STEPS):
                    if a is not None and s == LEAD + NT + 4:
                        dve.wait_ge(kv_acc, NT * (a + 1) + 2)
                        hm = headmask[:].rearrange("p h c -> p (h c)")
                        for r in range(2):
                            acc = bank[3 + r][:, 0:2 * (P + 1)].rearrange("p (g c) -> p g c", g=2)
                            ve_.tensor_tensor(kvd[:, 2 * r:2 * r + 2, 0:P], acc[:, :, 0:P],
                                              hm.unsqueeze(1).to_broadcast([P, 2, P]), ALU.mult)
                            last = ve_.tensor_tensor(kvd[:, 2 * r:2 * r + 2, P:P + HPG],
                                                     acc[:, :, P:P + 1].to_broadcast([P, 2, HPG]),
                                                     headmask[:, :, 0].unsqueeze(1).to_broadcast([P, 2, HPG]), ALU.mult)
                            last.then_inc(kvd_done, 1)
                    i = s - LEAD - 1
                    if due(a, i):
                        v = NT * a + i
                        dve.wait_ge(rstd_done, v + 1)
                        if i >= 2:
                            dve.wait_ge(xt_full, v - 1)
                        ve_.tensor_scalar(xn[:, i % 2, :], xb[:, i, :], mv[:, i % 2, 0:1], rstd[:, i % 2:i % 2 + 1],
                                          ALU.subtract, ALU.mult).then_inc(xn_done, 1)
                    i = s - LEAD
                    if due(a, i):
                        v = NT * a + i
                        dve.wait_ge(x_landed[i], 16 * (a + 1))
                        if i >= 2:
                            dve.wait_ge(xn_done, v - 1)
                        ve_.bn_stats(stats[:, i % 2, :], xb[:, i, :]).then_inc(stats_done, 1)
                        dve.wait_ge(stats_done, v + 1)
                        carry(dve)
                        ve_.bn_aggr(mv[:, i % 2, :], stats[:, i % 2, :]).then_inc(mv_done, 1)
                    i = s - 3
                    if due(n, i):
                        v = NT * n + i
                        dve.wait_ge(rstd2_done, v + 1)
                        dve.wait_ge(x1n_stored[i % 2], 16 * (NT // 2 * n + i // 2 + 1))
                        if i >= 2:
                            dve.wait_ge(nt_full, v - 1)
                        ve_.tensor_scalar(x1n[:, i % 2, :], x1[:, i % 2, :], mv2[:, 0:1], rstd2[:], ALU.subtract,
                                          ALU.mult).then_inc(x1n_done, 1)
                    i = s - 2
                    if due(n, i):
                        v = NT * n + i
                        dve.wait_ge(o_full, v + 1)
                        if i > 0:
                            dve.wait_ge(x1n_done, v)
                        dve.wait_ge(bo_added, v + 1)
                        dve.wait_ge(x1_stored[i % 2], 16 * (NT // 2 * n + i // 2 + 1))
                        ve_.tensor_tensor(x1[:, i % 2, :], bank[7][:], xb[:, i, :], ALU.add).then_inc(x1_done, 1)
                        dve.wait_ge(x1_done, v + 1)
                        ve_.bn_stats(stats2[:], x1[:, i % 2, :]).then_inc(stats2_done, 1)
                        dve.wait_ge(stats2_done, v + 1)
                        carry(dve)
                        ve_.bn_aggr(mv2[:], stats2[:]).then_inc(mv2_done, 1)
                    i = s - LEAD - 2
                    if due(a, i):
                        dve.wait_ge(xt_hi_done, NT * a + i + 1)
                        split_lo(bank[0], xt_lo[:, :, P * i:P * (i + 1)], xt_hi[:, :, P * i:P * (i + 1)], xt_lo_done)
                    for m_ in range(KC):
                        if n is None and s == MATRIX_STEPS[m_]:
                            matrix_lo(m_)
                    if n is None and s == LEAD + 2:
                        dve.wait_ge(small_landed, 80)
                    c = s - LEAD - 6
                    if due(a, c, QC):
                        v = QC * a + c
                        dve.wait_ge(qt_done, v + 2)
                        dve.wait_ge(qp_done, v + 1)
                        ve_.tensor_scalar(qe[:], qt[:], 0.0, None, ALU.min).then_inc(qm_done, 1)
                    c = s - LEAD - 6
                    if due(a, c, QC):
                        v = QC * a + c
                        dve.wait_ge(qe_done, v + 1)
                        ve_.scalar_tensor_tensor(out=qp[:, c % KC, 512 * (c // KC):512 * (c // KC + 1)], in0=qt[:],
                                                 scalar=0.0, in1=qe[:], op0=ALU.max, op1=ALU.add).then_inc(qp_done, 1)
                    i = s - LEAD - 3
                    if due(a, i):
                        v = NT * a + i
                        dve.wait_ge(v_full, v + 1)
                        dve.wait_ge(kv_acc, v + 1)
                        ve_.tensor_tensor(vx[:, i % 2, :, 0:P], bank[2][:].rearrange("p (g c) -> p g c", g=G),
                                          bvb[:].rearrange("p (g c) -> p g c", g=G), ALU.add).then_inc(v_done, 1)
                    i = s - LEAD - 3
                    if due(a, i):
                        v = NT * a + i
                        dve.wait_ge(k_full, v + 1)
                        dve.wait_ge(kp_done, v + 1)
                        ve_.tensor_tensor(kt[:], bank[1][:], bkb[:], ALU.add).then_inc(kt_done, 1)
                        dve.wait_ge(kt_done, v + 2)
                        ve_.tensor_scalar(ke[:], kt[:], 0.0, None, ALU.min).then_inc(km_done, 1)
                    i = s - 1
                    if due(n, i):
                        dve.wait_ge(att_hi_done, NT * n + i + 1)
                        split_lo(bank[7], at_lo[:, i % 2], at_hi[:, i % 2], att_lo_done)
                    i = s - LEAD - 3
                    if due(a, i):
                        v = NT * a + i
                        dve.wait_ge(ke_done, v + 1)
                        ve_.scalar_tensor_tensor(out=kp[:, i % 2, :], in0=kt[:], scalar=0.0, in1=ke[:],
                                                 op0=ALU.max, op1=ALU.add).then_inc(kp_done, 1)
                    i = s
                    if due(n, i):
                        v = NT * n + i
                        dve.wait_ge(num_full, v + 1)
                        dve.wait_ge(z_rec, v + 1)
                        sides = ((bank[6][:, 0:(G - 1) * W], slice(0, G - 1)), (bank[5][:, Z0:Z0 + W], slice(G - 1, G)))
                        for src, gs in sides:
                            ve_.tensor_scalar(zi[:, 0, gs, :], src.rearrange("p (g c) -> p g c", c=W)[:, :, P:W], Z_EPS,
                                              None, ALU.add).then_inc(z_read, 1)
                        dve.wait_ge(z_read, 2 * v + 2)
                        dve.wait_ge(at_done, v + 1)
                        ve_.reciprocal(zi[:, 1], zi[:, 0]).then_inc(z_rec, 1)
                        dve.wait_ge(z_rec, v + 2)
                        if i >= 2:
                            dve.wait_ge(att_full, v - 1)
                        for src, gs in sides:
                            ng = gs.stop - gs.start
                            ins = ve_.tensor_tensor(
                                at[:, i % 2, P * gs.start:P * gs.stop].rearrange("p (g h c) -> p g h c", h=HPG, c=HEAD_DIM),
                                src.rearrange("p (g c) -> p g c", c=W)[:, :, 0:P].rearrange("p g (h c) -> p g h c", h=HPG),
                                zi[:, 1, gs, :].unsqueeze(3).to_broadcast([P, ng, HPG, HEAD_DIM]), ALU.mult)
                        ins.then_inc(at_done, 1)
                    if n is not None and s == NT + 3:
                        route_logits(n)
                    if n is not None and s == NT + 4:
                        route_gates(n)
                    if n is not None and s == NT + 4:
                        route_choices(n)
                    if n is not None and s == NT + 5:
                        route_positions(n)
                    if n is not None and s in (NT + 6, NT + 7):
                        route_records(n, s - NT - 6)
                    if a is None and s in W1_STEPS:
                        w1_lo_part(0, W1_STEPS.index(s))

            PARTS = (2, 6, 8, NT + 4, 9, 8)

            def stepper(b, part):
                k = [ROUTE_STEPS * b + sum(PARTS[:part]), 0]

                def step(ins):
                    k[1] += 1
                    ins.then_inc(route, 1)
                    dve.wait_ge(route, k[0] + k[1])
                return step, k

            def col(c):
                return m[:, c, :]

            def wide(ap):
                return ap.unsqueeze(2).to_broadcast([P, NT, E])

            efw = ef[:].unsqueeze(1).to_broadcast([P, NT, E])

            def route_logits(b):
                step, k = stepper(b, 0)
                dve.wait_ge(lg_full, NT * (b + 1) + 1)
                step(ve_.tensor_copy(lg[:], bank[5][:, 0:R].rearrange("p (t e) -> p t e", e=E)))
                step(ve_.tensor_reduce(col(RM), lg[:], AX.X, ALU.max))
                ve_.tensor_tensor(gt[:], lg[:], wide(col(RM)), ALU.subtract).then_inc(lg_exp_in, 1)
                assert k[1] == PARTS[0]

            def choose(step, c):
                step(ve_.tensor_reduce(col(G1 + c), gt[:], AX.X, ALU.max))
                step(ve_.tensor_tensor(tmp[:], gt[:], wide(col(G1 + c)), ALU.not_equal))
                step(ve_.scalar_tensor_tensor(out=tmp[:], in0=tmp[:], scalar=float(E), in1=efw, op0=ALU.mult,
                                              op1=ALU.add))

            def route_gates(b):
                step, k = stepper(b, 1)
                dve.wait_ge(lg_exp, b + 1)
                step(ve_.tensor_reduce(col(RS), gt[:], AX.X, ALU.add))
                step(ve_.reciprocal(col(WS), col(RS)))
                step(ve_.tensor_tensor(gt[:], gt[:], wide(col(WS)), ALU.mult))
                choose(step, 0)
                assert k[1] == PARTS[1]

            def route_choices(b):
                step, k = stepper(b, 2)
                step(ve_.tensor_reduce(col(I1), tmp[:], AX.X, ALU.min))
                step(ve_.tensor_tensor(oh[:, 0], efw, wide(col(I1)), ALU.is_equal))
                step(ve_.scalar_tensor_tensor(out=gt[:], in0=oh[:, 0], scalar=-2.0, in1=gt[:], op0=ALU.mult,
                                              op1=ALU.add))
                choose(step, 1)
                step(ve_.tensor_reduce(col(I1), tmp[:], AX.X, ALU.min))
                step(ve_.tensor_tensor(oh[:, 1], efw, wide(col(I1)), ALU.is_equal))
                ve_.tensor_tensor(cnt[:], oh[:, 0], oh[:, 1], ALU.add).then_inc(cnt_done, 1)
                assert k[1] == PARTS[2]

            def route_positions(b):
                step, k = stepper(b, 3)
                step(ve_.tensor_copy(base[:, 0, :], base[:, NT, :]))
                dve.wait_ge(cum_full, b + 1)
                ve_.tensor_copy(cums[:].rearrange("p a r -> p (a r)"), bank[5][:, R:3 * R]).then_inc(cum_read, 1)
                dve.wait_ge(cum_read, b + 2)
                for t in range(NT):
                    step(ve_.tensor_tensor(base[:, t + 1, :], base[:, t, :], cums[:, 1, E * t:E * (t + 1)], ALU.add))
                step(ve_.tensor_tensor(pos[:], cums[:, 0, :].rearrange("p (t e) -> p t e", e=E), base[:, 0:NT, :],
                                       ALU.add))
                step(ve_.tensor_tensor(col(WS), col(G1), col(G2), ALU.add))
                step(ve_.tensor_scalar(col(WS), col(WS), W_EPS, None, ALU.add))
                assert k[1] == PARTS[3], k[1]

            def route_records(b, c):
                step, k = stepper(b, 4 + c)
                if c == 0:
                    dve.wait_ge(recs_free, b + 1)
                    step(ve_.reciprocal(col(WS), col(WS)))
                step(ve_.tensor_tensor(tmp[:], pos[:], oh[:, c], ALU.mult))
                step(ve_.tensor_reduce(col(SL), tmp[:], AX.X, ALU.add))
                step(ve_.tensor_scalar(col(VA), col(SL), float(CAP), float(SLOTS), ALU.is_ge, ALU.mult))
                step(ve_.tensor_tensor(col(SL), col(SL), col(VA), ALU.add))
                step(ve_.tensor_tensor(tmp[:], oh[:, c], ecap[:].unsqueeze(1).to_broadcast([P, NT, E]), ALU.mult))
                step(ve_.tensor_reduce(col(VA), tmp[:], AX.X, ALU.add))
                step(ve_.tensor_tensor(slot_i[:, c, :], col(SL), col(VA), ALU.add))
                step(ve_.tensor_tensor(rec[:, c, :, 1], col(G1 + c), col(WS), ALU.mult))
                ids = tok_id[:, bass.ds(b * NT, NT)]
                carry(dve)
                ve_.tensor_copy(rec[:, c, :, 0].bitcast(I32), ids).then_inc(rec_done, 1)
                assert k[1] == PARTS[4 + c], k[1]

            steps(0, None, LEAD)
            with dve.Fori(0, B - 1) as b:
                steps(b + 1, b)
            steps(None, B - 1)

            k = [0]

            def planning(ins):
                k[0] += 1
                ins.then_inc(planned, 1)
                dve.wait_ge(planned, k[0])

            rows_of = base[:, NT, :]
            planning(ve_.memset(plan_f[:], 0.0))
            for j in range(1, TPE):
                planning(ve_.scalar_tensor_tensor(out=plan_f[:, EXTRA, 0:E], in0=rows_of, scalar=float(j * TT),
                                                  in1=plan_f[:, EXTRA, 0:E], op0=ALU.is_gt, op1=ALU.add))
            planning(ve_.scalar_tensor_tensor(out=plan_f[:, BOTH, 0:E], in0=plan_f[:, EXTRA, 0:E], scalar=float(-TT),
                                              in1=rows_of, op0=ALU.mult, op1=ALU.add))
            planning(ve_.tensor_scalar(plan_f[:, BOTH, 0:E], plan_f[:, BOTH, 0:E], float(P), None, ALU.is_gt))
            for e in range(E):
                planning(ve_.scalar_tensor_tensor(out=plan_f[:, BEFORE, e + 1:e + 2], in0=plan_f[:, BEFORE, e:e + 1],
                                                  scalar=1.0, in1=plan_f[:, EXTRA, e:e + 1], op0=ALU.add, op1=ALU.add))
            planning(ve_.scalar_tensor_tensor(out=plan_f[:, BOTH, 0:E], in0=plan_f[:, EXTRA, 0:E], scalar=128.0,
                                              in1=plan_f[:, BOTH, 0:E], op0=ALU.mult, op1=ALU.add))
            planning(ve_.scalar_tensor_tensor(out=plan_f[:, BOTH, 0:E], in0=plan_f[:, BEFORE, 0:E], scalar=2.0,
                                              in1=plan_f[:, BOTH, 0:E], op0=ALU.mult, op1=ALU.add))
            ve_.tensor_copy(plan[:], plan_f[:, BOTH, 0:E]).then_inc(plan_ready, 1)
            dve.wait_ge(plan_ready, 1)
            for j in range(PAIRS):
                w2_lo_part(0, j)
            dve.drain().then_inc(phase_a, 1)

            def rows_lo(g):
                for c in range(2):
                    dve.wait_ge(et_split_hi, 2 * g + c + 1)
                    ve_.tensor_tensor(et_lo[:, 2 * c:2 * c + 2, :], et_bank[c][:].rearrange("p (c t) -> p c t", c=2),
                                      et_hi[:, 2 * c:2 * c + 2, :].bitcast(F32), ALU.subtract).then_inc(et_ready, 1)

            def y_bias(e, g):
                dve.wait_ge(b2_landed, 16 * (e + 1))
                dve.wait_ge(adds_done, g + 1)
                for h in range(HT):
                    dve.wait_ge(mm2_done, MC * (g + 1) + 4)
                    ve_.tensor_tensor(ys[:, h, :], y_bank[h][:], b2_cur[:], ALU.add).then_inc(y_read, 1)

            def tile(e, g, final, more):
                for mm in range(MC):
                    v = MC * g + mm
                    dve.wait_ge(h32_done, v + 5)
                    dve.wait_ge(mm2_done, v + 1)
                    ve_.tensor_copy(h_hi[:, mm % 4, :], h32[:, mm % 2, :]).then_inc(h_split_hi, 1)
                    dve.wait_ge(h_split_hi, v + 1)
                    ve_.tensor_tensor(h_lo[:, mm % 4, :], h32[:, mm % 2, :], h_hi[:, mm % 4, :].bitcast(F32),
                                      ALU.subtract).then_inc(h_ready, 1)
                    if final and more and mm % 2 == 1:
                        w1_lo_part(e + 1, mm // 2)
                    if final and more and mm % 2 == 0 and mm >= 4:
                        w2_lo_part(e + 1, mm // 2 - 2)
                if more or not final:
                    rows_lo(g + 1)
                if final and more:
                    w2_lo_part(e + 1, PAIRS - 2)
                y_bias(e, g)
                if final and more:
                    w2_lo_part(e + 1, PAIRS - 1)

            dve.wait_ge(phase_a, 4)
            ve_.memset(y_bank[1][:], 0.0).then_inc(y_cleared, 1)
            rows_lo(0)

            def expert(e, more):
                extra, before, _ = tiles_of(dve, e)
                with dve.Fori(0, TPE - 1) as t:
                    with dve.If(t < extra):
                        tile(e, before + t, False, more)
                tile(e, before + extra, True, more)

            with dve.Fori(0, E - 1) as e:
                expert(e, True)
            expert(E - 1, False)

        @block.tensor
        def _(pe):
            mm_ = nc.tensor.matmul
            pe.sem_inc(kv_acc, 2)
            pe.sem_inc(lg_full, 1)
            pe.sem_inc(mm2_done, 4)
            pe.sem_inc(et_full, 1)
            pe.wait_ge(const_done, 3)
            pe.wait_ge(dconst_done, 2)

            def product(out_, left, right, n, first=True, last=True):
                for c in range(n):
                    lh, ll = left(c)
                    rh, rl = right(c)
                    mm_(out_, lh, rh, start=(first and c == 0), stop=False)
                    mm_(out_, lh, rl, start=False, stop=False)
                    ins = mm_(out_, ll, rh, start=False, stop=(last and c == n - 1))
                return ins

            def turn(dst, src):
                for c in range(KC):
                    ins = nc.tensor.transpose(dst[:, P * c:P * (c + 1)], src[:, P * c:P * (c + 1)], ident[:])
                return ins

            def steps(a, n, first=0):
                for s in range(first, STEPS):
                    i = s - 2
                    if due(n, i):
                        v = NT * n + i
                        pe.wait_ge(st_lo, 4)
                        pe.wait_ge(att_lo_done, v + 1)
                        product(bank[7][:], lambda k: (at_hi[:, i % 2, k, :], at_lo[:, i % 2, k, :]),
                                lambda k: (whi["o"][:, k, :], wlo["o"][:, k, :]), KC).then_inc(o_full, 1)
                    i = s - LEAD - 2
                    if due(a, i):
                        v = NT * a + i
                        pe.wait_ge(xn_done, v + 1)
                        pe.wait_ge(xt_lo_done, v + 1)
                        if due(n, s - 4):
                            pe.wait_ge(nt_done, NT * n + s - 4 + 1)
                        turn(bank[0], xn[:, i % 2, :]).then_inc(xt_full, 1)
                    c = s - LEAD - 6
                    if due(a, c, QC):
                        v = QC * a + c
                        o, h = c % KC, c // KC
                        pe.wait_ge(st_lo, 3)
                        pe.wait_ge(xt_lo_done, NT * a + 4 * h + 5)
                        pe.wait_ge(qt_done, v + 1)
                        pe.wait_ge(kt_done, NT * a + min(c + 2, NT - 1) + 2)
                        product(bank[1][:], lambda k: (whi["q"][:, k, P * o:P * (o + 1)], wlo["q"][:, k, P * o:P * (o + 1)]),
                                lambda k: (xt_hi[:, k, 512 * h:512 * (h + 1)], xt_lo[:, k, 512 * h:512 * (h + 1)]),
                                KC).then_inc(q_full, 1)
                    i = s - LEAD - 3
                    toks = lambda k: (xt_hi[:, k, P * i:P * (i + 1)], xt_lo[:, k, P * i:P * (i + 1)])
                    if due(a, i):
                        v = NT * a + i
                        pe.wait_ge(st_lo, 1)
                        pe.wait_ge(xt_lo_done, v + 2)
                        pe.wait_ge(v_done, v + 1)
                        product(bank[2][:], toks, lambda k: (whi["v"][:, k, :], wlo["v"][:, k, :]), KC).then_inc(v_full, 1)
                    i = s - 4
                    if due(n, i):
                        pe.wait_ge(nt_done, NT * n + i + 1)
                        pe.wait_ge(at_done, NT * n + min(s, NT) + 1)
                        for k in range(KC):
                            ins = mm_(bank[5][:, E * i:E * (i + 1)], nt[:, k, :], gw[:, k, :], start=(k == 0),
                                      stop=(k == KC - 1))
                        ins.then_inc(lg_full, 1)
                    i = s - LEAD - 3
                    if due(a, i):
                        v = NT * a + i
                        pe.wait_ge(st_lo, 2)
                        pe.wait_ge(kt_done, v + 1)
                        if i >= 3:
                            pe.wait_ge(qt_done, QC * a + i - 3 + 2)
                        product(bank[1][:], toks, lambda k: (whi["k"][:, k, :], wlo["k"][:, k, :]), KC).then_inc(k_full, 1)
                    i = s - 1
                    if due(n, i):
                        v = NT * n + i
                        pe.wait_ge(at_done, v + 2)
                        if i > 0:
                            pe.wait_ge(x1_done, v)
                        turn(bank[7], at[:, i % 2, :]).then_inc(att_full, 1)
                    if n is not None and s == NT + 5:
                        pe.wait_ge(cnt_done, n + 1)
                        c2 = cnt[:].rearrange("p t e -> p (t e)")
                        mm_(bank[5][:, R:2 * R], upper[:], c2, start=True, stop=True)
                        mm_(bank[5][:, 2 * R:3 * R], ones[:], c2, start=True, stop=True).then_inc(cum_full, 1)
                    i = s - LEAD - 4
                    if due(a, i):
                        v = NT * a + i
                        pe.wait_ge(kp_done, v + 2)
                        pe.wait_ge(v_done, v + 2)
                        for g in range(G):
                            dst = bank[3 + g // 2][:, (P + 1) * (g % 2):(P + 1) * (g % 2 + 1)]
                            ins = mm_(dst, kp[:, i % 2, P * g:P * (g + 1)], vx[:, i % 2, g, :],
                                      start=(i == 0 and g % 2 == 0), stop=(i == NT - 1), skip_group_check=True)
                        ins.then_inc(kv_acc, 1)
                    i = s
                    if due(n, i):
                        v = NT * n + i
                        pe.wait_ge(kvd_done, 2 * (n + 1))
                        pe.wait_ge(qp_done, QC * n + KC * (i // 4 + 1) + 1)
                        pe.wait_ge(at_done, v + 1)
                        if i == 0:
                            pe.wait_ge(cum_read, n + 1)
                        for g in range(G):
                            q_ = qp[:, g, P * i:P * (i + 1)]
                            dst = bank[6][:, W * g:W * (g + 1)] if g < G - 1 else bank[5][:, Z0:Z0 + W]
                            ins = mm_(dst, q_, kvd[:, g, :], start=True, stop=True)
                        ins.then_inc(num_full, 1)
                    i = s - 3
                    if due(n, i):
                        v = NT * n + i
                        pe.wait_ge(x1n_done, v + 1)
                        if i > 0:
                            pe.wait_ge(nt_done, v)
                        if due(a, s - LEAD - 2):
                            pe.wait_ge(xt_lo_done, NT * a + s - LEAD - 2 + 2)
                        turn(bank[0], x1n[:, i % 2, :]).then_inc(nt_full, 1)

            steps(0, None, LEAD)
            with pe.Fori(0, B - 1) as b:
                steps(b + 1, b)
            steps(None, B - 1)
            pe.drain().then_inc(phase_a, 1)

            def rows(g):
                for h in range(HT):
                    pe.wait_ge(gathered[h], 16 * (g + 1))
                if not (isinstance(g, int) and g == 0):
                    pe.wait_ge(et_ready, 2 * g)
                for c in range(2):
                    for k in range(2):
                        for h in range(HT):
                            ins = nc.tensor.transpose(et_bank[c][:, TT * k + P * h:TT * k + P * (h + 1)],
                                                      xg[:, h, P * (2 * c + k):P * (2 * c + k + 1)], ident[:])
                    ins.then_inc(et_full, 1)

            def tile(e, g, more, halves=HT):
                for mm in range(MC + LAG):
                    if mm < MC:
                        if mm % 2 == 0:
                            pe.wait_ge(w1_ready, PAIRS * e + mm // 2 + 1 + RING)
                        pe.wait_ge(h32_done, MC * g + mm + 1)
                        if mm == 0:
                            pe.wait_ge(et_ready, 2 * g + 2)
                        cols = slice(P * mm, P * (mm + 1))
                        product(h_bank[mm % 4][:, 0:TT], lambda k: (w1_hi[:, k, cols], w1_lo[:, k, cols]),
                                lambda k: (et_hi[:, k, :], et_lo[:, k, :]), KC).then_inc(h_full, 1)
                    if mm == MC // 2 and more:
                        rows(g + 1)
                    n = mm - LAG
                    if n >= 0:
                        if n % 2 == 0:
                            pe.wait_ge(w2_ready, PAIRS * e + n // 2 + 1 + RING)
                        pe.wait_ge(h_ready, MC * g + n + 3)
                        if n == 0:
                            pe.wait_ge(y_read, HT * g + 1)
                        for h in range(halves):
                            toks = slice(P * h, P * (h + 1))
                            ins = product(y_bank[h][:], lambda k: (h_hi[:, n % 4, toks], h_lo[:, n % 4, toks]),
                                          lambda k: (w2_hi[:, n, :], w2_lo[:, n, :]), 1, first=(n == 0),
                                          last=(n == MC - 1))
                        ins.then_inc(mm2_done, 1)

            pe.wait_ge(phase_a, 4)
            rows(0)
            pe.wait_ge(y_cleared, 1)

            def expert(e, more):
                extra, before, both = tiles_of(pe, e)
                with pe.Fori(0, TPE - 1) as t:
                    with pe.If(t < extra):
                        tile(e, before + t, True)
                with pe.If(both > 0):
                    tile(e, before + extra, more)
                with pe.If(both < 1):
                    tile(e, before + extra, more, halves=1)

            with pe.Fori(0, E - 1) as e:
                expert(e, True)
            expert(E - 1, False)


_INS = ["hidden_states", "q_w", "q_b", "k_w", "k_b", "v_w", "v_b", "o_w", "o_b"]
_FFN = ["gating_w", "w1", "b1", "w2", "b2"]


def kernel(**inputs):
    import numpy as _np
    import concourse.bacc as _bacc
    from concourse import mybir as _mybir
    from concourse.bass_utils import run_bass_kernel_spmd as _run

    nc = _bacc.Bacc("TRN2", target_bir_lowering=False, num_devices=1)
    arrays, args = {}, []
    for name in [f"L0_attn_{n}" for n in _INS] + [f"L0_ffn_{n}" for n in _FFN]:
        a = _np.asarray(inputs[name])
        if name in ("L0_attn_q_w", "L0_attn_k_w", "L0_attn_v_w", "L0_attn_o_w"):
            a = a.T
        a = _np.ascontiguousarray(a)
        arrays[f"{name}_dram"] = a
        args.append(nc.dram_tensor(f"{name}_dram", a.shape, _mybir.dt.from_np(a.dtype), kind="ExternalInput").ap())
    x = inputs["L0_attn_hidden_states"]
    b, s, d = x.shape
    out = nc.dram_tensor("out_dram", (b * s + PAD, d), _mybir.dt.float32, kind="ExternalOutput").ap()
    moe_block(nc, *args, out)
    r = _run(nc, [arrays], core_ids=[0])
    return r.results[0]["out_dram"][0:b * s].reshape(b, s, d)
```
